# Optimizing a Trainium2 kernel written in Bass

```python
import numpy as np
import jax
import jax.numpy as jnp

def _softmax(x, axis=-1):
    return jax.nn.softmax(x, axis=axis)

def _gelu(x):
    return jax.nn.gelu(x, approximate=True)

def _silu(x):
    return jax.nn.silu(x)

def _sigmoid(x):
    return jax.nn.sigmoid(x)

def _layernorm(x, axis=-1, eps=1e-05):
    m = jnp.mean(x, axis=axis, keepdims=True)
    v = jnp.var(x, axis=axis, keepdims=True)
    return (x - m) / jnp.sqrt(v + eps)

def _scatter_add(tgt, idx, src, axis=0):
    return tgt.at[idx].add(src)

def _segment_sum(src, seg, n):
    return jax.ops.segment_sum(src, seg, n)
kernel_name = 'mk_seq_postln_d1_jaxref_r8_f21b35'

def setup_inputs(seed: int=0):
    np.random.seed(seed)
    _w = jnp.asarray

    def _L0_attn_setup():
        import jax, jax.numpy as jnp
        import numpy as np
        D = 128
        key = jax.random.key(seed)
        ks = jax.random.split(key, 9)
        s = 1.0 / np.sqrt(D)
        x = jax.random.normal(ks[0], (8, 512, D), dtype=jnp.float32)
        Wq = jax.random.uniform(ks[1], (D, D), jnp.float32, -s, s)
        bq = jax.random.uniform(ks[2], (D,), jnp.float32, -s, s)
        Wk = jax.random.uniform(ks[3], (D, D), jnp.float32, -s, s)
        bk = jax.random.uniform(ks[4], (D,), jnp.float32, -s, s)
        Wv = jax.random.uniform(ks[5], (D, D), jnp.float32, -s, s)
        bv = jax.random.uniform(ks[6], (D,), jnp.float32, -s, s)
        Wo = jax.random.uniform(ks[7], (D, D), jnp.float32, -s, s)
        bo = jax.random.uniform(ks[8], (D,), jnp.float32, -s, s)
        return {'x': x, 'Wq': Wq, 'bq': bq, 'Wk': Wk, 'bk': bk, 'Wv': Wv, 'bv': bv, 'Wo': Wo, 'bo': bo}
    _L0_attn_in = _L0_attn_setup()

    def _L0_ffn_setup():
        import jax, jax.numpy as jnp
        import numpy as np
        from jax import lax
        T, B, I, M, O = (32, 64, 128, 128, 128)

        def _xavier(key, shape):
            fan_out, fan_in = shape
            limit = float(np.sqrt(6.0 / (fan_in + fan_out)))
            return jax.random.uniform(key, shape, jnp.float32, -limit, limit)
        key = jax.random.key(seed)
        ks = jax.random.split(key, 9)
        x = jax.random.normal(ks[0], (T, B, I), jnp.float32)
        return {'x': x, 'wf': _xavier(ks[1], (M, I)), 'uf': _xavier(ks[2], (M, M)), 'bf': jnp.zeros((M,), jnp.float32), 'wi': _xavier(ks[3], (M, I)), 'ui': _xavier(ks[4], (M, M)), 'bi': jnp.zeros((M,), jnp.float32), 'wc': _xavier(ks[5], (M, I)), 'uc': _xavier(ks[6], (M, M)), 'bc': jnp.zeros((M,), jnp.float32), 'wo': _xavier(ks[7], (O, I)), 'uo': _xavier(ks[8], (O, M)), 'bo': jnp.zeros((O,), jnp.float32), 'in_c': jnp.zeros((M,), jnp.float32)}
    _L0_ffn_in = _L0_ffn_setup()
    _d = {'L0_attn_x': _L0_attn_in['x'], 'L0_attn_Wq': _L0_attn_in['Wq'], 'L0_attn_bq': _L0_attn_in['bq'], 'L0_attn_Wk': _L0_attn_in['Wk'], 'L0_attn_bk': _L0_attn_in['bk'], 'L0_attn_Wv': _L0_attn_in['Wv'], 'L0_attn_bv': _L0_attn_in['bv'], 'L0_attn_Wo': _L0_attn_in['Wo'], 'L0_attn_bo': _L0_attn_in['bo'], 'L0_ffn_wf': _L0_ffn_in['wf'], 'L0_ffn_uf': _L0_ffn_in['uf'], 'L0_ffn_bf': _L0_ffn_in['bf'], 'L0_ffn_wi': _L0_ffn_in['wi'], 'L0_ffn_ui': _L0_ffn_in['ui'], 'L0_ffn_bi': _L0_ffn_in['bi'], 'L0_ffn_wc': _L0_ffn_in['wc'], 'L0_ffn_uc': _L0_ffn_in['uc'], 'L0_ffn_bc': _L0_ffn_in['bc'], 'L0_ffn_wo': _L0_ffn_in['wo'], 'L0_ffn_uo': _L0_ffn_in['uo'], 'L0_ffn_bo': _L0_ffn_in['bo'], 'L0_ffn_in_c': _L0_ffn_in['in_c']}
    _x0 = _d['L0_attn_x']
    _d['L0_attn_x'] = jax.random.normal(jax.random.fold_in(jax.random.key(seed), 1), (8, 512, 128), dtype=_x0.dtype)
    del _x0
    return _d

def reference(L0_attn_x, L0_attn_Wq, L0_attn_bq, L0_attn_Wk, L0_attn_bk, L0_attn_Wv, L0_attn_bv, L0_attn_Wo, L0_attn_bo, L0_ffn_wf, L0_ffn_uf, L0_ffn_bf, L0_ffn_wi, L0_ffn_ui, L0_ffn_bi, L0_ffn_wc, L0_ffn_uc, L0_ffn_bc, L0_ffn_wo, L0_ffn_uo, L0_ffn_bo, L0_ffn_in_c):

    def _L0_attn_ref(x, Wq, bq, Wk, bk, Wv, bv, Wo, bo):
        import jax, jax.numpy as jnp
        import numpy as np
        D = 128
        Q = x @ Wq.T + bq
        K = x @ Wk.T + bk
        V = x @ Wv.T + bv
        Q = jax.nn.elu(Q) + 1.0
        K = jax.nn.elu(K) + 1.0
        KV = jnp.einsum('bnd,bne->bde', K, V)
        Z = jnp.einsum('bnd,bd->bn', Q, K.sum(axis=1) + 1e-06)
        context = jnp.einsum('bnd,bde->bne', Q, KV) / Z[..., None]
        return context @ Wo.T + bo

    def _L0_ffn_ref(x, wf, uf, bf, wi, ui, bi, wc, uc, bc, wo, uo, bo, in_c):
        import jax, jax.numpy as jnp
        import numpy as np
        from jax import lax
        T, B, I, M, O = (32, 64, 128, 128, 128)

        def _xavier(key, shape):
            fan_out, fan_in = shape
            limit = float(np.sqrt(6.0 / (fan_in + fan_out)))
            return jax.random.uniform(key, shape, jnp.float32, -limit, limit)
        batch = x.shape[1]
        c0 = jnp.broadcast_to(in_c, (batch, in_c.shape[0]))

        def step(c, xt):
            ft = jax.nn.sigmoid(xt @ wf.T + c @ uf.T + bf)
            it = jax.nn.sigmoid(xt @ wi.T + c @ ui.T + bi)
            gt = jnp.tanh(xt @ wc.T + c @ uc.T + bc)
            c = ft * c + it * gt
            return (c, None)
        c_final, _ = lax.scan(step, c0, x)
        h = jnp.tanh(jnp.einsum('tbi,oi->tbo', x, wo) + c_final @ uo.T + bo)
        return h
    x = L0_attn_x
    x = _layernorm(x + _L0_attn_ref(x, L0_attn_Wq, L0_attn_bq, L0_attn_Wk, L0_attn_bk, L0_attn_Wv, L0_attn_bv, L0_attn_Wo, L0_attn_bo), axis=-1)
    x = _layernorm(x + _L0_ffn_ref(x, L0_ffn_wf, L0_ffn_uf, L0_ffn_bf, L0_ffn_wi, L0_ffn_ui, L0_ffn_bi, L0_ffn_wc, L0_ffn_uc, L0_ffn_bc, L0_ffn_wo, L0_ffn_uo, L0_ffn_bo, L0_ffn_in_c), axis=-1)
    return x

_drawn_inputs = setup_inputs


def setup_inputs(seed=0):
    import zlib

    import numpy as np

    out = dict(_drawn_inputs(seed))
    spreads = {'L0_ffn_bf': (0.0, 0.731),
     'L0_ffn_bi': (0.0, 0.698),
     'L0_ffn_bc': (0.0, 0.1),
     'L0_ffn_bo': (0.0, 0.1),
     'L0_ffn_in_c': (0.0, 0.8)}
    factors = {'L0_attn_Wq': 8.0,
     'L0_attn_bq': 8.0,
     'L0_attn_Wk': 8.0,
     'L0_attn_bk': 8.0,
     'L0_attn_Wv': 3.843}
    for name, (base, spread) in spreads.items():
        noise = np.random.default_rng([zlib.crc32(name.encode()), seed]).standard_normal(out[name].shape)
        drawn = base * np.exp(spread * noise) if base else spread * noise
        out[name] = jnp.asarray(drawn.astype(out[name].dtype))
    for name, factor in factors.items():
        out[name] = (out[name] * factor).astype(out[name].dtype)
    return out
```

```python
from contextlib import ExitStack

import concourse.bass as bass
from concourse import mybir

ALU = mybir.AluOpType
ACT = mybir.ActivationFunctionType
F32 = mybir.dt.float32
F32R = mybir.dt.float32r

T = 8
N = 512
D = 128
C = N // D
DZ = D + 1
LN_EPS = 1e-5
Z_EPS = 1e-6

WK_T, WQ_T, WV, WO_T = range(4)
GATES = 3
BQ, BF, BI, BC, C0, BV = range(6)
BK_ROW, BOUT_ROW, BATT_ROW = range(3)


def build(nc, x, xt, w_att, w_gate, w_out, cols, rows, out):
    with ExitStack() as ctx:
        def sb(name, shape, dt=F32):
            return ctx.enter_context(nc.sbuf_tensor(name, shape, dt))

        def bank(name):
            return ctx.enter_context(nc.psum_tensor(name, [D, N], F32))

        def sem(name):
            return ctx.enter_context(nc.semaphore(name))

        x_rows = sb("x_rows", [D, T, C, D])
        x_cols = sb("x_cols", [D, T, C, D])
        ones_col = sb("ones_col", [D, 1])
        watt = sb("watt", [D, 4, D])
        wgate = sb("wgate", [D, 2 * GATES, D])
        wout = sb("wout", [D, 2, D])
        col = sb("col", [D, 6])
        row = sb("row", [D, 3, D])

        ident = sb("ident", [D, D])
        ones_r = sb("ones_r", [D, D], F32R)
        minus_half = sb("minus_half", [D, C])
        minus_one = sb("minus_one", [D, 1])
        bq1 = sb("bq1", [D, 1])
        half_b = sb("half_b", [D, 2])
        s0 = sb("s0", [D, 1])
        first_b = sb("first_b", [D, GATES])
        wgate_hi = sb("wgate_hi", [D, 2 * GATES, D], F32R)
        wgate_lo = sb("wgate_lo", [D, 2 * GATES, D], F32R)
        uo_half = sb("uo_half", [D, D])
        bv_wide = sb("bv_wide", [D, D])
        w_vo = sb("w_vo", [D, D])
        bias_z = sb("bias_z", [D, DZ])
        eps_z = sb("eps_z", [D, DZ])
        row_hi = sb("row_hi", [D, 2, D], F32R)
        row_lo = sb("row_lo", [D, 2, D], F32R)
        row_t = sb("row_t", [D, 2, D])
        row_parts = sb("row_parts", [D, 2, D], F32R)

        k_exp = sb("k_exp", [D, 2, C, D])
        k_rows = sb("k_rows", [D, 2, C, D])
        q_exp = sb("q_exp", [D, 2, N])
        q_min = sb("q_min", [D, 2, N])
        q_cols = sb("q_cols", [D, 2, C, D])
        kx = sb("kx", [D, 2, DZ])
        kx_t = sb("kx_t", [D, 2, D])
        kvo = sb("kvo", [D, 2, DZ])
        z_inv = sb("z_inv", [D, 2, C])
        x1 = sb("x1", [D, T, C, D])
        stats = sb("stats", [D, 2, C, 6])
        mean_var = sb("mean_var", [D, 2, C, 2])
        var_eps = sb("var_eps", [D, 2, C])
        rstd = sb("rstd", [D, 2, C])
        x1_cols = sb("x1_cols", [D, T, C, D])
        x1_hi = sb("x1_hi", [D, 2, N], F32R)
        x1_lo = sb("x1_lo", [D, 2, N], F32R)
        th_f = sb("th_f", [D, N])
        th_i = sb("th_i", [D, N])
        th_c = sb("th_c", [D, N])
        keep = sb("keep", [D, N])
        new = sb("new", [D, N])
        s = sb("s", [D, 2, C, D])
        s_hi = sb("s_hi", [D, 2, N], F32R)
        s_lo = sb("s_lo", [D, 2, N], F32R)
        h_rows = sb("h_rows", [D, 2, C, D])

        ps_k, ps_q = bank("ps_k"), bank("ps_q")
        ps_f, ps_i, ps_c = bank("ps_f"), bank("ps_i"), bank("ps_c")
        ps_x1 = bank("ps_x1")
        ps_ctx = ctx.enter_context(nc.psum_tensor("ps_ctx", [D, 2, N], F32))
        ctx_view = ps_ctx[:, :, 0:2 * DZ].rearrange("p b (c d) -> p b c d", d=DZ)
        small = ps_ctx[:, 1, 2 * DZ:3 * DZ]
        out_banks = [ps_k[:], ps_q[:], ps_x1[:], ps_ctx[:, 0, :], ps_ctx[:, 1, :], ps_f[:], ps_i[:], ps_c[:]]

        att_in, gate_in, out_in, vec_in = sem("att_in"), sem("gate_in"), sem("out_in"), sem("vec_in")
        x_in = [sem(f"x_in{t}") for t in range(T)]
        ident_ok, ones_ok, pool_c = sem("ident_ok"), sem("ones_ok"), sem("pool_c")
        vecs_ok, rows_ok, dve_c = sem("vecs_ok"), sem("rows_ok"), sem("dve_c")
        split_hi, split_lo = sem("split_hi"), sem("split_lo")
        setup_mm, bias_z_ok, w_vo_ok, first_b_ok = sem("setup_mm"), sem("bias_z_ok"), sem("w_vo_ok"), sem("first_b_ok")
        k_mm, k_exp_ok, k_ok = sem("k_mm"), sem("k_exp_ok"), sem("k_ok")
        q_mm, q_exp_ok, q_min_ok, q_ok = sem("q_mm"), sem("q_exp_ok"), sem("q_min_ok"), sem("q_ok")
        kx_mm, kx_ok, kxt_mm, kxt_ok = sem("kx_mm"), sem("kx_ok"), sem("kxt_mm"), sem("kxt_ok")
        kvo_mm, kvo_b, kvo_ok = sem("kvo_mm"), sem("kvo_b"), sem("kvo_ok")
        ctx_mm, z_ok, y_ok = sem("ctx_mm"), sem("z_ok"), sem("y_ok")
        st_ok, agg_ok, var_ok, rstd_ok, x1_ok = sem("st_ok"), sem("agg_ok"), sem("var_ok"), sem("rstd_ok"), sem("x1_ok")
        x1t_mm, x1c_ok, x1hi_ok, x1lo_ok = sem("x1t_mm"), sem("x1c_ok"), sem("x1hi_ok"), sem("x1lo_ok")
        f_mm, i_mm, c_mm = sem("f_mm"), sem("i_mm"), sem("c_mm")
        f_ok, i_ok, c_ok = sem("f_ok"), sem("i_ok"), sem("c_ok")
        keep_ok, new_ok, s_ok, shi_ok, slo_ok = sem("keep_ok"), sem("new_ok"), sem("s_ok"), sem("shi_ok"), sem("slo_ok")
        out_mm, h_ok, w_ok, y2_ok, stored = sem("out_mm"), sem("h_ok"), sem("w_ok"), sem("y2_ok"), sem("stored")

        block = ctx.enter_context(nc.Block())

        def rows_of(dram, t):
            return dram[t].rearrange("(p c) d -> p c d", c=C)

        def periods():
            def inside(v):
                return v if 0 <= v < T else None
            for n in range(T + 2):
                yield inside(n), inside(n - 1), inside(n - 2)

        @block.sync
        def _(sp):
            sp.dma_start(x_cols[:, 0], xt[0]).then_inc(x_in[0], 16)
            sp.dma_start(x_rows[:, 0], rows_of(x, 0)).then_inc(x_in[0], 16)
            sp.dma_start(wgate[:], w_gate).then_inc(gate_in, 16)
            for t in range(1, T):
                sp.dma_start(x_cols[:, t], xt[t]).then_inc(x_in[t], 16)
                sp.dma_start(x_rows[:, t], rows_of(x, t)).then_inc(x_in[t], 16)
                if t == 1:
                    sp.dma_start(wout[:], w_out).then_inc(out_in, 16)
            for t in range(T):
                sp.wait_ge(y2_ok, t + 1)
                sp.dma_start(rows_of(out, t), x1[:, t]).then_inc(stored, 16)
            sp.wait_ge(stored, 16 * T)

        @block.gpsimd
        def _(pool):
            nc.gpsimd.memset(ident[:], 0.0).then_inc(pool_c, 1)
            nc.gpsimd.memset(ones_r[:].bitcast(F32), 1.0).then_inc(ones_ok, 1)
            nc.gpsimd.memset(ones_col[:], 1.0).then_inc(ones_ok, 1)
            nc.gpsimd.memset(minus_half[:], -0.5).then_inc(ones_ok, 1)
            nc.gpsimd.memset(minus_one[:], -1.0).then_inc(ones_ok, 1)
            pool.wait_ge(pool_c, 1)
            nc.gpsimd.affine_select(out=ident[:], in_=ident[:], compare_op=ALU.not_equal, fill=1.0, base=0,
                                    pattern=[[-1, D]], channel_multiplier=1).then_inc(ident_ok, 1)
            pool.wait_ge(ones_ok, 4)

            def reciprocal_root(n):
                pool.wait_ge(var_ok, n + 1)
                nc.gpsimd.tensor_tensor(rstd[:, n % 2], var_eps[:, n % 2], minus_half[:], ALU.pow).then_inc(rstd_ok, 1)

            for n, (a, b, t) in enumerate(periods()):
                if t is not None and t >= 1:
                    pool.wait_ge(shi_ok, t)
                    nc.gpsimd.tensor_tensor(s_lo[:, (t - 1) % 2], s[:, (t - 1) % 2].rearrange("p c d -> p (c d)"),
                                            s_hi[:, (t - 1) % 2].bitcast(F32), ALU.subtract).then_inc(slo_ok, 1)
                if b is not None:
                    reciprocal_root(b)
                if a is not None:
                    pool.wait_ge(q_exp_ok, a + 1)
                    nc.gpsimd.tensor_scalar(q_min[:, a % 2], q_exp[:, a % 2], 1.0, 0.0, ALU.min, ALU.add).then_inc(q_min_ok, 1)
            for t in range(T):
                reciprocal_root(T + t)

        @block.tensor
        def _(pe):
            def keys(a):
                if a == 0:
                    pe.wait_ge(att_in, 16)
                pe.wait_ge(x_in[a], 32)
                if a >= 1:
                    pe.wait_ge(k_exp_ok, a)
                    pe.wait_ge(k_ok, a)
                for c in range(C):
                    nc.tensor.matmul(ps_k[:, c * D:(c + 1) * D], x_cols[:, a, c], watt[:, WK_T],
                                     start=(c == 0), stop=False, skip_group_check=True)
                if a == 0:
                    pe.wait_ge(rows_ok, 1)
                    pe.wait_ge(ones_ok, 4)
                nc.tensor.matmul(ps_k[:], ones_r[:], row_parts[:, BK_ROW].unsqueeze(1).to_broadcast([D, C, D]),
                                 start=False, stop=True, skip_group_check=True).then_inc(k_mm, 1)

            def queries(a):
                if a >= 1:
                    pe.wait_ge(q_exp_ok, a)
                    pe.wait_ge(q_ok, a)
                nc.tensor.matmul(ps_q[:], watt[:, WQ_T], x_cols[:, a].rearrange("p c d -> p (c d)"),
                                 start=True, stop=True).then_inc(q_mm, 1)

            def keys_x(a):
                pe.wait_ge(k_ok, a + 1)
                if a >= 1:
                    pe.wait_ge(y_ok, a)
                for c in range(C):
                    nc.tensor.matmul(small[:, 0:D], k_rows[:, a % 2, c], x_rows[:, a, c],
                                     start=(c == 0), stop=(c == C - 1), skip_group_check=True)
                for c in range(C):
                    mm = nc.tensor.matmul(small[:, D:DZ], k_rows[:, a % 2, c], ones_col[:],
                                          start=False, stop=(c == C - 1), skip_group_check=True)
                mm.then_inc(kx_mm, 1)

            def keys_x_turned(a):
                if a == 0:
                    pe.wait_ge(ident_ok, 1)
                pe.wait_ge(kx_ok, a + 1)
                nc.tensor.transpose(small[:, 0:D], kx[:, a % 2, 0:D], ident[:]).then_inc(kxt_mm, 1)

            def key_values(a):
                if a == 0:
                    pe.wait_ge(w_vo_ok, 1)
                pe.wait_ge(kxt_ok, a + 1)
                nc.tensor.matmul(small[:, 0:D], kx_t[:, a % 2], w_vo[:], start=True, stop=True).then_inc(kvo_mm, 1)

            def context(b):
                pe.wait_ge(q_ok, b + 1)
                pe.wait_ge(kvo_ok, b + 1)
                if b >= 1:
                    pe.wait_ge(y_ok, b)
                for c in range(C):
                    mm = nc.tensor.matmul(ctx_view[:, c // 2, c % 2], q_cols[:, b % 2, c], kvo[:, b % 2],
                                          start=True, stop=True, skip_group_check=True)
                mm.then_inc(ctx_mm, 1)

            def x1_turned(b):
                pe.wait_ge(x1_ok, b + 1)
                if b >= 1:
                    pe.wait_ge(x1c_ok, b)
                for c in range(C):
                    mm = nc.tensor.transpose(ps_x1[:, c * D:(c + 1) * D], x1[:, b, c], ident[:])
                mm.then_inc(x1t_mm, 1)

            def gate(ps, g, t, used, done):
                if t == 0:
                    pe.wait_ge(split_lo, 1)
                if t >= 1:
                    pe.wait_ge(used, t)
                pe.wait_ge(x1hi_ok, t + 1)
                parts = [(wgate_hi[:, g], x1_hi[:, t % 2]), (wgate_lo[:, g], x1_hi[:, t % 2]),
                         (wgate_hi[:, g], x1_lo[:, t % 2])]
                if t >= 1:
                    u = GATES + g
                    last = (t - 1) % 2
                    parts += [(wgate_hi[:, u], s_hi[:, last]), (wgate_lo[:, u], s_hi[:, last]),
                              (wgate_hi[:, u], s_lo[:, last])]
                for n, (w, v) in enumerate(parts):
                    if n == 2:
                        pe.wait_ge(x1lo_ok, t + 1)
                    if n == 3:
                        pe.wait_ge(shi_ok, t)
                    if n == 5:
                        pe.wait_ge(slo_ok, t)
                    mm = nc.tensor.matmul(ps[:], w, v, start=(n == 0), stop=(n == len(parts) - 1))
                mm.then_inc(done, 1)

            def setup():
                pe.wait_ge(vecs_ok, 1)
                nc.tensor.matmul(ps_i[:, 0:D], watt[:, WV], watt[:, WO_T], start=True, stop=True,
                                 skip_group_check=True).then_inc(setup_mm, 1)
                nc.tensor.matmul(ps_x1[:, 0:D], bv_wide[:], watt[:, WO_T], start=True, stop=True,
                                 skip_group_check=True).then_inc(setup_mm, 1)
                pe.wait_ge(gate_in, 16)
                for g in range(GATES):
                    mm = nc.tensor.matmul(ps_c[:, g:g + 1], wgate[:, GATES + g], col[:, C0:C0 + 1],
                                          start=True, stop=True, skip_group_check=True)
                mm.then_inc(setup_mm, 1)

            for a, b, t in periods():
                if b is not None:
                    context(b)
                if a is not None:
                    keys(a)
                    if a == 0:
                        setup()
                    queries(a)
                if t is not None:
                    gate(ps_f, 0, t, f_ok, f_mm)
                if a is not None:
                    keys_x(a)
                if t is not None:
                    gate(ps_i, 1, t, i_ok, i_mm)
                if a is not None:
                    keys_x_turned(a)
                if t is not None:
                    gate(ps_c, 2, t, c_ok, c_mm)
                if a is not None:
                    key_values(a)
                if b is not None:
                    x1_turned(b)

            pe.wait_ge(out_in, 16)
            pe.wait_ge(x1c_ok, T)
            for t in range(T):
                ps = out_banks[t]
                if t >= T - GATES:
                    pe.wait_ge([f_ok, i_ok, c_ok][t - (T - GATES)], T)
                for c in range(C):
                    nc.tensor.matmul(ps[:, c * D:(c + 1) * D], x1_cols[:, t, c], wout[:, 0],
                                     start=(c == 0), stop=False, skip_group_check=True)
                nc.tensor.matmul(ps, ones_r[:], row_parts[:, BOUT_ROW].unsqueeze(1).to_broadcast([D, C, D]),
                                 start=False, stop=False, skip_group_check=True)
            pe.wait_ge(s_ok, T)
            for t in range(T):
                ps = out_banks[t]
                for c in range(C):
                    mm = nc.tensor.matmul(ps[:, c * D:(c + 1) * D], s[:, (T - 1) % 2, c], uo_half[:],
                                          start=False, stop=(c == C - 1), skip_group_check=True)
                mm.then_inc(out_mm, 1)

        @block.scalar
        def _(act):
            act.dma_start(watt[:], w_att).then_inc(att_in, 16)
            act.dma_start(col[:], cols).then_inc(vec_in, 16)
            act.dma_start(row[:], rows.partition_broadcast(D)).then_inc(vec_in, 16)

            def key_exp(a):
                act.wait_ge(k_mm, a + 1)
                nc.scalar.activation(k_exp[:, a % 2].rearrange("p c d -> p (c d)"), ps_k[:], ACT.Exp,
                                     bias=minus_one[:, 0:1]).then_inc(k_exp_ok, 1)

            def query_exp(a):
                act.wait_ge(q_mm, a + 1)
                nc.scalar.activation(q_exp[:, a % 2], ps_q[:], ACT.Exp, bias=col[:, BQ:BQ + 1]).then_inc(q_exp_ok, 1)

            def tanh(ps, done, t, made, out_tile, scale, bias, ok):
                act.wait_ge(done, t + 1)
                if t >= 1:
                    act.wait_ge(made, t)
                nc.scalar.activation(out_tile[:], ps[:], ACT.Tanh, bias=bias, scale=scale).then_inc(ok, 1)

            for a, b, t in periods():
                if t is not None and t >= 1:
                    act.wait_ge(s_ok, t)
                    nc.scalar.activation(s_hi[:, (t - 1) % 2], s[:, (t - 1) % 2].rearrange("p c d -> p (c d)"),
                                         ACT.Copy).then_inc(shi_ok, 1)
                if a is not None:
                    if a == 0:
                        act.wait_ge(vec_in, 32)
                        act.wait_ge(ones_ok, 4)
                    key_exp(a)
                    if a == 0:
                        act.wait_ge(setup_mm, 1)
                        nc.scalar.activation(w_vo[:], ps_i[:, 0:D], ACT.Copy).then_inc(w_vo_ok, 1)
                    query_exp(a)
                if t is not None:
                    tanh(ps_f, f_mm, t, keep_ok, th_f, 0.5, half_b[:, 0:1] if t else first_b[:, 0:1], f_ok)
                if a is not None:
                    act.wait_ge(kx_mm, a + 1)
                    nc.scalar.activation(kx[:, a % 2], small[:], ACT.Copy).then_inc(kx_ok, 1)
                    if a == 0:
                        act.wait_ge(gate_in, 16)
                        nc.scalar.activation(wgate_hi[:, 0:GATES], wgate[:, 0:GATES], ACT.Copy)
                        nc.scalar.activation(wgate_hi[:, GATES:2 * GATES], wgate[:, GATES:2 * GATES], ACT.Copy,
                                             scale=0.5).then_inc(split_hi, 1)
                if t is not None:
                    tanh(ps_i, i_mm, t, new_ok, th_i, 0.5, half_b[:, 1:2] if t else first_b[:, 1:2], i_ok)
                if a is not None:
                    act.wait_ge(kxt_mm, a + 1)
                    nc.scalar.activation(kx_t[:, a % 2], small[:, 0:D], ACT.Copy).then_inc(kxt_ok, 1)
                if t is not None:
                    tanh(ps_c, c_mm, t, new_ok, th_c, 1.0, col[:, BC:BC + 1] if t else first_b[:, 2:3], c_ok)
                if b is not None:
                    act.wait_ge(x1t_mm, b + 1)
                    nc.scalar.activation(x1_cols[:, b].rearrange("p c d -> p (c d)"), ps_x1[:],
                                         ACT.Copy).then_inc(x1c_ok, 1)
                    act.wait_ge(x1c_ok, b + 1)
                    nc.scalar.activation(x1_hi[:, b % 2], x1_cols[:, b].rearrange("p c d -> p (c d)"),
                                         ACT.Copy).then_inc(x1hi_ok, 1)
            for t in range(T):
                act.wait_ge(out_mm, t + 1)
                if t >= 2:
                    act.wait_ge(w_ok, t - 1)
                nc.scalar.activation(h_rows[:, t % 2].rearrange("p c d -> p (c d)"), out_banks[t], ACT.Tanh).then_inc(h_ok, 1)

        @block.vector
        def _(dve):
            def setup():
                dve.wait_ge(vec_in, 32)
                nc.vector.memset(bias_z[:], 1.0).then_inc(dve_c, 1)
                nc.vector.memset(eps_z[:], Z_EPS).then_inc(dve_c, 1)
                nc.vector.tensor_scalar(row_t[:, BK_ROW], row[:, BK_ROW], 1.0, None, ALU.add).then_inc(dve_c, 1)
                nc.vector.tensor_copy(row_t[:, BOUT_ROW], row[:, BOUT_ROW]).then_inc(dve_c, 1)
                nc.vector.tensor_scalar(bq1[:], col[:, BQ:BQ + 1], 1.0, None, ALU.add).then_inc(dve_c, 1)
                nc.vector.tensor_scalar(half_b[:], col[:, BF:BI + 1], 0.5, None, ALU.mult).then_inc(dve_c, 1)
                nc.vector.tensor_scalar(s0[:], col[:, C0:C0 + 1], 2.0, None, ALU.mult).then_inc(dve_c, 1)
                dve.wait_ge(dve_c, 4)
                nc.vector.tensor_copy(row_hi[:], row_t[:]).then_inc(dve_c, 1)
                dve.wait_ge(dve_c, 8)
                nc.vector.tensor_tensor(row_lo[:], row_t[:], row_hi[:].bitcast(F32), ALU.subtract).then_inc(dve_c, 1)
                dve.wait_ge(dve_c, 9)
                dve.wait_ge(ident_ok, 1)
                nc.vector.tensor_scalar(row_t[:], row_hi[:].bitcast(F32), ident[:, 0:1], None, ALU.mult).then_inc(dve_c, 1)
                dve.wait_ge(dve_c, 10)
                nc.vector.scalar_tensor_tensor(row_parts[:], row_lo[:].bitcast(F32), ident[:, 1:2], row_t[:],
                                               ALU.mult, ALU.add).then_inc(rows_ok, 1)
                dve.wait_ge(ones_ok, 4)
                nc.vector.tensor_scalar(bv_wide[:], ones_r[:].bitcast(F32), col[:, BV:BV + 1], None,
                                        ALU.mult).then_inc(vecs_ok, 1)
                nc.vector.tensor_scalar(eps_z[:, 0:D], row[:, BATT_ROW], Z_EPS, None, ALU.mult).then_inc(dve_c, 1)

            def setup_products():
                dve.wait_ge(setup_mm, 2)
                nc.vector.tensor_tensor(bias_z[:, 0:D], ps_x1[:, 0:D], row[:, BATT_ROW], ALU.add).then_inc(bias_z_ok, 1)
                dve.wait_ge(setup_mm, 3)
                nc.vector.tensor_tensor(first_b[:], ps_c[:, 0:GATES], col[:, BF:BC + 1], ALU.add).then_inc(first_b_ok, 1)
                dve.wait_ge(first_b_ok, 1)
                nc.vector.tensor_scalar(first_b[:, 0:2], first_b[:, 0:2], 0.5, None, ALU.mult).then_inc(first_b_ok, 1)

            def split_low():
                dve.wait_ge(split_hi, 1)
                nc.vector.tensor_tensor(wgate_lo[:, 0:GATES], wgate[:, 0:GATES], wgate_hi[:, 0:GATES].bitcast(F32),
                                        ALU.subtract)
                g = slice(GATES, 2 * GATES)
                nc.vector.scalar_tensor_tensor(
                    wgate_lo[:, g].rearrange("p g d -> p (g d)"), wgate[:, g].rearrange("p g d -> p (g d)"), 0.5,
                    wgate_hi[:, g].rearrange("p g d -> p (g d)").bitcast(F32), ALU.mult, ALU.subtract).then_inc(split_lo, 1)
                dve.wait_ge(out_in, 16)
                nc.vector.tensor_scalar(uo_half[:], wout[:, 1], 0.5, None, ALU.mult).then_inc(dve_c, 1)

            def statistics(n, tile):
                for c in range(C):
                    st = nc.vector.bn_stats(stats[:, n % 2, c], tile[:, c])
                st.then_inc(st_ok, 1)
                dve.wait_ge(st_ok, n + 1)
                for c in range(C):
                    ag = nc.vector.bn_aggr(mean_var[:, n % 2, c], stats[:, n % 2, c])
                ag.then_inc(agg_ok, 1)
                dve.wait_ge(agg_ok, n + 1)
                nc.vector.tensor_scalar(var_eps[:, n % 2], mean_var[:, n % 2, :, 1], LN_EPS, None,
                                        ALU.add).then_inc(var_ok, 1)

            def normalise(n, tile, done):
                dve.wait_ge(rstd_ok, n + 1)
                for c in range(C):
                    ins = nc.vector.tensor_scalar(tile[:, c], tile[:, c], mean_var[:, n % 2, c, 0:1],
                                                  rstd[:, n % 2, c:c + 1], ALU.subtract, ALU.mult)
                ins.then_inc(done, 1)

            def residual(b):
                dve.wait_ge(ctx_mm, b + 1)
                nc.vector.reciprocal(z_inv[:, b % 2].rearrange("p (b c) -> p b c", c=2),
                                     ctx_view[:, :, :, D]).then_inc(z_ok, 1)
                dve.wait_ge(z_ok, b + 1)
                for c in range(C):
                    ins = nc.vector.scalar_tensor_tensor(x1[:, b, c], ctx_view[:, c // 2, c % 2, 0:D],
                                                         z_inv[:, b % 2, c:c + 1], x_rows[:, b, c], ALU.mult, ALU.add)
                ins.then_inc(y_ok, 1)
                dve.wait_ge(y_ok, b + 1)
                statistics(b, x1[:, b])

            setup()
            for a, b, t in periods():
                if b is not None:
                    residual(b)
                if a is not None:
                    dve.wait_ge(k_exp_ok, a + 1)
                    nc.vector.scalar_tensor_tensor(k_rows[:, a % 2], k_exp[:, a % 2], 1.0,
                                                   ps_k[:].rearrange("p (c d) -> p c d", d=D), ALU.min,
                                                   ALU.max).then_inc(k_ok, 1)
                    if a == 0:
                        setup_products()
                    dve.wait_ge(q_min_ok, a + 1)
                    nc.vector.scalar_tensor_tensor(q_cols[:, a % 2].rearrange("p c d -> p (c d)"), ps_q[:], bq1[:, 0:1],
                                                   q_min[:, a % 2], ALU.add, ALU.max).then_inc(q_ok, 1)
                if b is not None:
                    normalise(b, x1[:, b], x1_ok)
                if t is not None:
                    dve.wait_ge(f_ok, t + 1)
                    if t == 0:
                        nc.vector.tensor_scalar(keep[:], th_f[:], 1.0, s0[:, 0:1], ALU.add, ALU.mult).then_inc(keep_ok, 1)
                    else:
                        nc.vector.scalar_tensor_tensor(keep[:], th_f[:], 1.0, s[:, (t - 1) % 2].rearrange("p c d -> p (c d)"),
                                                       ALU.add, ALU.mult).then_inc(keep_ok, 1)
                if a is not None:
                    dve.wait_ge(kx_ok, a + 1)
                    if a == 0:
                        dve.wait_ge(bias_z_ok, 1)
                    nc.vector.scalar_tensor_tensor(kvo[:, a % 2], bias_z[:], kx[:, a % 2, D:DZ], eps_z[:],
                                                   ALU.mult, ALU.add).then_inc(kvo_b, 1)
                    if a == 0:
                        split_low()
                    dve.wait_ge(kvo_b, a + 1)
                    dve.wait_ge(kvo_mm, a + 1)
                    nc.vector.tensor_tensor(kvo[:, a % 2, 0:D], kvo[:, a % 2, 0:D], small[:, 0:D],
                                            ALU.add).then_inc(kvo_ok, 1)
                if t is not None:
                    dve.wait_ge(i_ok, t + 1)
                    dve.wait_ge(c_ok, t + 1)
                    nc.vector.scalar_tensor_tensor(new[:], th_i[:], 1.0, th_c[:], ALU.add, ALU.mult).then_inc(new_ok, 1)
                    dve.wait_ge(keep_ok, t + 1)
                    dve.wait_ge(new_ok, t + 1)
                    nc.vector.scalar_tensor_tensor(s[:, t % 2].rearrange("p c d -> p (c d)"), keep[:], 0.5, new[:],
                                                   ALU.mult, ALU.add).then_inc(s_ok, 1)
                if b is not None:
                    dve.wait_ge(x1hi_ok, b + 1)
                    nc.vector.tensor_tensor(x1_lo[:, b % 2], x1_cols[:, b].rearrange("p c d -> p (c d)"), x1_hi[:, b % 2].bitcast(F32),
                                            ALU.subtract).then_inc(x1lo_ok, 1)
            for t in range(T):
                dve.wait_ge(h_ok, t + 1)
                nc.vector.tensor_tensor(x1[:, t], x1[:, t], h_rows[:, t % 2], ALU.add).then_inc(w_ok, 1)
                dve.wait_ge(w_ok, t + 1)
                statistics(T + t, x1[:, t])
                if t >= 1:
                    normalise(T + t - 1, x1[:, t - 1], y2_ok)
            normalise(2 * T - 1, x1[:, T - 1], y2_ok)


def kernel(**inputs):
    import numpy as np
    import concourse.bacc as bacc
    from concourse.bass_utils import run_bass_kernel_spmd

    i = {name.removeprefix("L0_"): np.asarray(a) for name, a in inputs.items()}
    x = np.ascontiguousarray(i["attn_x"])
    xt = np.ascontiguousarray(x.reshape(T, D, C, D).transpose(0, 3, 2, 1))

    def packed(*mats):
        return np.ascontiguousarray(np.stack(mats, axis=1))

    arrays = {
        "x": x,
        "xt": xt,
        "w_att": packed(i["attn_Wk"].T, i["attn_Wq"].T, i["attn_Wv"], i["attn_Wo"].T),
        "w_gate": packed(*(i["ffn_" + n].T for n in ("wf", "wi", "wc", "uf", "ui", "uc"))),
        "w_out": packed(i["ffn_wo"].T, i["ffn_uo"].T),
        "cols": packed(i["attn_bq"], i["ffn_bf"], i["ffn_bi"], i["ffn_bc"], i["ffn_in_c"], i["attn_bv"]),
        "rows": np.ascontiguousarray(np.stack([i["attn_bk"], i["ffn_bo"], i["attn_bo"]])),
    }
    nc = bacc.Bacc("TRN2", target_bir_lowering=False, num_devices=1)
    aps = [nc.dram_tensor(n, a.shape, F32, kind="ExternalInput").ap() for n, a in arrays.items()]
    out = nc.dram_tensor("out", (T, N, D), F32, kind="ExternalOutput").ap()
    build(nc, *aps, out)
    return run_bass_kernel_spmd(nc, [arrays], core_ids=[0]).results[0]["out"]
```

```python
from contextlib import ExitStack

import concourse.bass as bass
from concourse import mybir

ALU = mybir.AluOpType
ACT = mybir.ActivationFunctionType
F32 = mybir.dt.float32
F32R = mybir.dt.float32r

T = 8
N = 512
D = 128
C = N // D
DZ = D + 1
DVE_CHUNKS = 2
WC = 2
LN_EPS = 1e-5
Z_EPS = 1e-6

WK_T, WQ_T, WV, WO_T = range(4)
GATES = 3
BQ, BF, BI, BC, C0, BV = range(6)
BK_ROW, BOUT_ROW, BATT_ROW = range(3)


def build(nc, x, xt, w_att, w_gate, w_out, cols, rows, out):
    with ExitStack() as ctx:
        def sb(name, shape, dt=F32):
            return ctx.enter_context(nc.sbuf_tensor(name, shape, dt))

        def bank(name):
            return ctx.enter_context(nc.psum_tensor(name, [D, N], F32))

        def sem(name):
            return ctx.enter_context(nc.semaphore(name))

        x_rows = sb("x_rows", [D, T, C, DZ])
        x_cols = sb("x_cols", [D, T, C, D])
        watt = sb("watt", [D, 4, D])
        wgate = sb("wgate", [D, 2 * GATES, D])
        wout = sb("wout", [D, 2, D])
        col = sb("col", [D, 6])
        row = sb("row", [D, 3, D])

        ident = sb("ident", [D, D])
        ones_r = sb("ones_r", [D, D], F32R)
        minus_half = sb("minus_half", [D, C])
        minus_one = sb("minus_one", [D, 1])
        half_b = sb("half_b", [D, 2])
        s0 = sb("s0", [D, 1])
        first_b = sb("first_b", [D, GATES])
        wgate_hi = sb("wgate_hi", [D, 2 * GATES, D], F32R)
        wgate_lo = sb("wgate_lo", [D, 2 * GATES, D], F32R)
        uo_half = sb("uo_half", [D, D])
        bv_wide = sb("bv_wide", [D, D])
        w_vo = sb("w_vo", [D, D])
        bias_z = sb("bias_z", [D, DZ])
        eps_z = sb("eps_z", [D, DZ])
        row_hi = sb("row_hi", [D, 2, D], F32R)
        row_lo = sb("row_lo", [D, 2, D], F32R)
        row_t = sb("row_t", [D, 2, D])
        row_parts = sb("row_parts", [D, 2, D], F32R)

        k_exp = sb("k_exp", [D, 2, C, D])
        k_rows = sb("k_rows", [D, 2, C, D])
        q_exp = sb("q_exp", [D, 2, N])
        q_relu = sb("q_relu", [D, 2, N])
        q_cols = sb("q_cols", [D, 2, C, D])
        kx = sb("kx", [D, 2, DZ])
        kx_t = sb("kx_t", [D, 2, D])
        kvo = sb("kvo", [D, 2, DZ])
        z_inv = sb("z_inv", [D, 2, C])
        x1 = sb("x1", [D, T, C, D])
        stats = sb("stats", [D, 4, C, 6])
        mean_var = sb("mean_var", [D, 4, C, 2])
        var_eps = sb("var_eps", [D, 4, C])
        neg_mean = sb("neg_mean", [D, 4, C])
        rstd = sb("rstd", [D, 4, C])
        shift = sb("shift", [D, 4, C])
        x1_cols = sb("x1_cols", [D, T, C, D])
        x1_hi = sb("x1_hi", [D, 2, N], F32R)
        x1_lo = sb("x1_lo", [D, 2, N], F32R)
        th_f = sb("th_f", [D, N])
        th_i = sb("th_i", [D, N])
        th_c = sb("th_c", [D, N])
        keep = sb("keep", [D, N])
        new = sb("new", [D, N])
        s = sb("s", [D, 2, C, D])
        s_hi = sb("s_hi", [D, 2, N], F32R)
        s_lo = sb("s_lo", [D, 2, N], F32R)
        h_rows = sb("h_rows", [D, 2, C, D])

        ps_k, ps_q = bank("ps_k"), bank("ps_q")
        ps_f, ps_i, ps_c = bank("ps_f"), bank("ps_i"), bank("ps_c")
        ps_x1 = bank("ps_x1")
        ps_ctx = ctx.enter_context(nc.psum_tensor("ps_ctx", [D, 2, N], F32))
        ctx_view = ps_ctx[:, :, 0:2 * DZ].rearrange("p b (c d) -> p b c d", d=DZ)
        small = ps_ctx[:, 1, 2 * DZ:3 * DZ]
        out_banks = [ps_k[:], ps_q[:], ps_ctx[:, 0, :], ps_ctx[:, 1, :], ps_x1[:], ps_f[:], ps_i[:], ps_c[:]]

        att_in, gate_in, out_in, vec_in = sem("att_in"), sem("gate_in"), sem("out_in"), sem("vec_in")
        x_in = [sem(f"x_in{t}") for t in range(T)]
        ident_ok, ones_ok, pool_c = sem("ident_ok"), sem("ones_ok"), sem("pool_c")
        vecs_ok, rows_ok, dve_c = sem("vecs_ok"), sem("rows_ok"), sem("dve_c")
        split_hi, split_lo = sem("split_hi"), sem("split_lo")
        setup_mm, bias_z_ok, w_vo_ok, first_b_ok = sem("setup_mm"), sem("bias_z_ok"), sem("w_vo_ok"), sem("first_b_ok")
        k_mm, k_exp_ok, k_ok = sem("k_mm"), sem("k_exp_ok"), sem("k_ok")
        q_mm, q_exp_ok, q_relu_ok, q_ok = sem("q_mm"), sem("q_exp_ok"), sem("q_relu_ok"), sem("q_ok")
        kx_mm, kx_ok, kxt_mm, kxt_ok = sem("kx_mm"), sem("kx_ok"), sem("kxt_mm"), sem("kxt_ok")
        kvo_mm, kvo_b, kvo_ok = sem("kvo_mm"), sem("kvo_b"), sem("kvo_ok")
        ctx_mm, z_ok, y_ok = sem("ctx_mm"), sem("z_ok"), sem("y_ok")
        st_ok, agg_ok, var_ok, rstd_ok, x1_ok = sem("st_ok"), sem("agg_ok"), sem("var_ok"), sem("rstd_ok"), sem("x1_ok")
        shift_ok, x1_act_ok = sem("shift_ok"), sem("x1_act_ok")
        x1t_mm, x1c_ok, x1hi_ok, x1lo_ok = sem("x1t_mm"), sem("x1c_ok"), sem("x1hi_ok"), sem("x1lo_ok")
        f_mm, i_mm, c_mm = sem("f_mm"), sem("i_mm"), sem("c_mm")
        f_ok, i_ok, c_ok = sem("f_ok"), sem("i_ok"), sem("c_ok")
        keep_ok, new_ok, s_ok, shi_ok, slo_ok = sem("keep_ok"), sem("new_ok"), sem("s_ok"), sem("shi_ok"), sem("slo_ok")
        out_mm, h_ok, w_ok, y2_ok, stored = sem("out_mm"), sem("h_ok"), sem("w_ok"), sem("y2_ok"), sem("stored")
        y2_act_ok, wp_ok = sem("y2_act_ok"), sem("wp_ok")

        block = ctx.enter_context(nc.Block())

        def rows_of(dram, t):
            return dram[t].rearrange("(p c) d -> p c d", c=C)

        def periods():
            def inside(v):
                return v if 0 <= v < T else None
            for n in range(T + 2):
                yield inside(n), inside(n - 1), inside(n - 2)

        @block.sync
        def _(sp):
            sp.dma_start(x_cols[:, 0], xt[0]).then_inc(x_in[0], 16)
            sp.dma_start(x_rows[:, 0, :, 0:D], rows_of(x, 0)).then_inc(x_in[0], 16)
            sp.dma_start(wgate[:], w_gate).then_inc(gate_in, 16)
            for t in range(1, T):
                sp.dma_start(x_cols[:, t], xt[t]).then_inc(x_in[t], 16)
                sp.dma_start(x_rows[:, t, :, 0:D], rows_of(x, t)).then_inc(x_in[t], 16)
                if t == 1:
                    sp.dma_start(wout[:], w_out).then_inc(out_in, 16)
            for t in range(T):
                sp.wait_ge(y2_ok, t + 1)
                sp.wait_ge(y2_act_ok, t + 1)
                sp.dma_start(rows_of(out, t), x1[:, t]).then_inc(stored, 16)
            sp.wait_ge(stored, 16 * T)

        @block.gpsimd
        def _(pool):
            nc.gpsimd.memset(ident[:], 0.0).then_inc(pool_c, 1)
            nc.gpsimd.memset(ones_r[:].bitcast(F32), 1.0).then_inc(ones_ok, 1)
            nc.gpsimd.memset(x_rows[:, :, :, D:DZ].rearrange("p t c d -> p (t c) d"), 1.0).then_inc(ones_ok, 1)
            nc.gpsimd.memset(minus_half[:], -0.5).then_inc(ones_ok, 1)
            nc.gpsimd.memset(minus_one[:], -1.0).then_inc(ones_ok, 1)
            pool.wait_ge(pool_c, 1)
            nc.gpsimd.affine_select(out=ident[:], in_=ident[:], compare_op=ALU.not_equal, fill=1.0, base=0,
                                    pattern=[[-1, D]], channel_multiplier=1).then_inc(ident_ok, 1)
            pool.wait_ge(ones_ok, 4)

            def reciprocal_root(n):
                pool.wait_ge(var_ok, 2 * n + 2)
                nc.gpsimd.tensor_tensor(rstd[:, n % 4], var_eps[:, n % 4], minus_half[:], ALU.pow).then_inc(rstd_ok, 1)
                pool.wait_ge(rstd_ok, n + 1)
                nc.gpsimd.tensor_tensor(shift[:, n % 4], neg_mean[:, n % 4], rstd[:, n % 4], ALU.mult).then_inc(shift_ok, 1)

            for n, (a, b, t) in enumerate(periods()):
                if t is not None and t >= 1:
                    pool.wait_ge(shi_ok, t)
                    nc.gpsimd.tensor_tensor(s_lo[:, (t - 1) % 2], s[:, (t - 1) % 2].rearrange("p c d -> p (c d)"),
                                            s_hi[:, (t - 1) % 2].bitcast(F32), ALU.subtract).then_inc(slo_ok, 1)
                if b is not None:
                    reciprocal_root(b)
            for t in range(T + 1):
                if t < T:
                    pool.wait_ge(h_ok, t + 1)
                    nc.gpsimd.tensor_tensor(x1[:, t, WC:], x1[:, t, WC:], h_rows[:, t % 2, WC:], ALU.add).then_inc(wp_ok, 1)
                if t >= 1:
                    reciprocal_root(T + t - 1)

        @block.tensor
        def _(pe):
            def keys(a):
                if a == 0:
                    pe.wait_ge(att_in, 16)
                pe.wait_ge(x_in[a], 32)
                if a >= 1:
                    pe.wait_ge(k_exp_ok, a)
                    pe.wait_ge(k_ok, a)
                for c in range(C):
                    nc.tensor.matmul(ps_k[:, c * D:(c + 1) * D], x_cols[:, a, c], watt[:, WK_T],
                                     start=(c == 0), stop=False, skip_group_check=True)
                if a == 0:
                    pe.wait_ge(rows_ok, 1)
                    pe.wait_ge(ones_ok, 4)
                nc.tensor.matmul(ps_k[:], ones_r[:], row_parts[:, BK_ROW].unsqueeze(1).to_broadcast([D, C, D]),
                                 start=False, stop=True, skip_group_check=True).then_inc(k_mm, 1)

            def queries(a):
                if a >= 1:
                    pe.wait_ge(q_relu_ok, a)
                nc.tensor.matmul(ps_q[:], watt[:, WQ_T], x_cols[:, a].rearrange("p c d -> p (c d)"),
                                 start=True, stop=True).then_inc(q_mm, 1)

            def keys_x(a):
                pe.wait_ge(k_ok, a + 1)
                if a >= 1:
                    pe.wait_ge(y_ok, a)
                for c in range(C):
                    mm = nc.tensor.matmul(small[:], k_rows[:, a % 2, c], x_rows[:, a, c],
                                          start=(c == 0), stop=(c == C - 1))
                mm.then_inc(kx_mm, 1)

            def keys_x_turned(a):
                if a == 0:
                    pe.wait_ge(ident_ok, 1)
                pe.wait_ge(kx_ok, a + 1)
                nc.tensor.transpose(small[:, 0:D], kx[:, a % 2, 0:D], ident[:]).then_inc(kxt_mm, 1)

            def key_values(a):
                if a == 0:
                    pe.wait_ge(w_vo_ok, 1)
                pe.wait_ge(kxt_ok, a + 1)
                nc.tensor.matmul(small[:, 0:D], kx_t[:, a % 2], w_vo[:], start=True, stop=True).then_inc(kvo_mm, 1)

            def context(b):
                pe.wait_ge(q_ok, b + 1)
                pe.wait_ge(kvo_ok, b + 1)
                if b >= 1:
                    pe.wait_ge(y_ok, b)
                for c in range(C):
                    mm = nc.tensor.matmul(ctx_view[:, c // 2, c % 2], q_cols[:, b % 2, c], kvo[:, b % 2],
                                          start=True, stop=True, skip_group_check=True)
                mm.then_inc(ctx_mm, 1)

            def x1_turned(b):
                pe.wait_ge(x1_ok, b + 1)
                pe.wait_ge(x1_act_ok, b + 1)
                if b >= 1:
                    pe.wait_ge(x1c_ok, b)
                for c in range(C):
                    mm = nc.tensor.transpose(ps_x1[:, c * D:(c + 1) * D], x1[:, b, c], ident[:])
                mm.then_inc(x1t_mm, 1)

            def gate_x(ps, g, t, used, done):
                if t == 0:
                    pe.wait_ge(split_lo, 1)
                if t >= 1:
                    pe.wait_ge(used, t)
                pe.wait_ge(x1hi_ok, t + 1)
                nc.tensor.matmul(ps[:], wgate_hi[:, g], x1_hi[:, t % 2], start=True, stop=False)
                nc.tensor.matmul(ps[:], wgate_lo[:, g], x1_hi[:, t % 2], start=False, stop=False)
                pe.wait_ge(x1lo_ok, t + 1)
                mm = nc.tensor.matmul(ps[:], wgate_hi[:, g], x1_lo[:, t % 2], start=False, stop=(t == 0))
                if t == 0:
                    mm.then_inc(done, 1)

            def gate_s(ps, g, t, done):
                if t >= 1:
                    u, last = GATES + g, (t - 1) % 2
                    pe.wait_ge(shi_ok, t)
                    nc.tensor.matmul(ps[:], wgate_hi[:, u], s_hi[:, last], start=False, stop=False)
                    nc.tensor.matmul(ps[:], wgate_lo[:, u], s_hi[:, last], start=False, stop=False)
                    pe.wait_ge(slo_ok, t)
                    nc.tensor.matmul(ps[:], wgate_hi[:, u], s_lo[:, last], start=False, stop=True).then_inc(done, 1)

            def out_x(t):
                ps = out_banks[t]
                if t == 0:
                    pe.wait_ge(out_in, 16)
                    pe.wait_ge(q_relu_ok, T)
                    pe.wait_ge(k_ok, T)
                    pe.wait_ge(x1c_ok, T - 2)
                if t == 2:
                    pe.wait_ge(y_ok, T)
                if t == 4:
                    pe.wait_ge(x1c_ok, T)
                if t >= T - GATES:
                    pe.wait_ge([f_ok, i_ok, c_ok][t - (T - GATES)], T)
                for c in range(C):
                    nc.tensor.matmul(ps[:, c * D:(c + 1) * D], x1_cols[:, t, c], wout[:, 0],
                                     start=(c == 0), stop=False, skip_group_check=True)
                nc.tensor.matmul(ps, ones_r[:], row_parts[:, BOUT_ROW].unsqueeze(1).to_broadcast([D, C, D]),
                                 start=False, stop=False, skip_group_check=True)

            def out_s(t):
                if t == 0:
                    pe.wait_ge(s_ok, T)
                for c in range(C):
                    mm = nc.tensor.matmul(out_banks[t][:, c * D:(c + 1) * D], s[:, (T - 1) % 2, c], uo_half[:],
                                          start=False, stop=(c == C - 1), skip_group_check=True)
                mm.then_inc(out_mm, 1)

            def setup():
                pe.wait_ge(vecs_ok, 1)
                nc.tensor.matmul(ps_i[:, 0:D], watt[:, WV], watt[:, WO_T], start=True, stop=True,
                                 skip_group_check=True).then_inc(setup_mm, 1)
                nc.tensor.matmul(ps_x1[:, 0:D], bv_wide[:], watt[:, WO_T], start=True, stop=True,
                                 skip_group_check=True).then_inc(setup_mm, 1)
                pe.wait_ge(gate_in, 16)
                for g in range(GATES):
                    mm = nc.tensor.matmul(ps_c[:, g:g + 1], wgate[:, GATES + g], col[:, C0:C0 + 1],
                                          start=True, stop=True, skip_group_check=True)
                mm.then_inc(setup_mm, 1)

            for a, b, t in periods():
                if a is not None:
                    keys(a)
                    if a == 0:
                        setup()
                    queries(a)
                if t == T - 1:
                    out_x(1)
                    out_x(2)
                if t is not None:
                    gate_x(ps_f, 0, t, f_ok, f_mm)
                    gate_x(ps_i, 1, t, i_ok, i_mm)
                    gate_x(ps_c, 2, t, c_ok, c_mm)
                if a is not None:
                    keys_x(a)
                if t is not None:
                    gate_s(ps_f, 0, t, f_mm)
                if a is not None:
                    keys_x_turned(a)
                if t is not None:
                    gate_s(ps_i, 1, t, i_mm)
                if a is not None:
                    key_values(a)
                if t is not None:
                    gate_s(ps_c, 2, t, c_mm)
                if a is not None:
                    context(a)
                if t == T - 2:
                    out_x(0)
                if b is not None:
                    x1_turned(b)
            out_x(3)
            out_x(4)
            for t in range(T):
                out_s(t)
                if t + 5 < T:
                    out_x(t + 5)

        @block.scalar
        def _(act):
            act.dma_start(watt[:], w_att).then_inc(att_in, 16)
            act.dma_start(col[:], cols).then_inc(vec_in, 16)
            act.dma_start(row[:], rows.partition_broadcast(D)).then_inc(vec_in, 16)

            def key_exp(a):
                act.wait_ge(k_mm, a + 1)
                nc.scalar.activation(k_exp[:, a % 2].rearrange("p c d -> p (c d)"), ps_k[:], ACT.Exp,
                                     bias=minus_one[:, 0:1]).then_inc(k_exp_ok, 1)

            def query_exp(a):
                act.wait_ge(q_mm, a + 1)
                nc.scalar.activation(q_exp[:, a % 2], ps_q[:], ACT.Exp, bias=col[:, BQ:BQ + 1]).then_inc(q_exp_ok, 1)
                nc.scalar.activation(q_relu[:, a % 2], ps_q[:], ACT.Relu, bias=col[:, BQ:BQ + 1]).then_inc(q_relu_ok, 1)

            def tanh(ps, done, t, made, out_tile, scale, bias, ok):
                act.wait_ge(done, t + 1)
                if t >= 1:
                    act.wait_ge(made, t)
                nc.scalar.activation(out_tile[:], ps[:], ACT.Tanh, bias=bias, scale=scale).then_inc(ok, 1)

            def normalise(n, tile, done, chunks):
                act.wait_ge(shift_ok, n + 1)
                for c in range(chunks, C):
                    ins = nc.scalar.activation(tile[:, c], tile[:, c], ACT.Identity, bias=shift[:, n % 4, c:c + 1],
                                               scale=rstd[:, n % 4, c:c + 1])
                ins.then_inc(done, 1)

            def x1_high(b):
                act.wait_ge(x1t_mm, b + 1)
                nc.scalar.activation(x1_hi[:, b % 2], ps_x1[:], ACT.Copy).then_inc(x1hi_ok, 1)

            def x1_whole(b):
                act.wait_ge(x1lo_ok, b + 1)
                nc.scalar.activation(x1_cols[:, b].rearrange("p c d -> p (c d)"), ps_x1[:],
                                     ACT.Copy).then_inc(x1c_ok, 1)

            for a, b, t in periods():
                if b is not None and b >= 1:
                    x1_high(b - 1)
                if t is not None and t >= 1:
                    act.wait_ge(s_ok, t)
                    nc.scalar.activation(s_hi[:, (t - 1) % 2], s[:, (t - 1) % 2].rearrange("p c d -> p (c d)"),
                                         ACT.Copy).then_inc(shi_ok, 1)
                if a is not None:
                    if a == 0:
                        act.wait_ge(vec_in, 32)
                        act.wait_ge(ones_ok, 4)
                    key_exp(a)
                    if a == 0:
                        act.wait_ge(setup_mm, 1)
                        nc.scalar.activation(w_vo[:], ps_i[:, 0:D], ACT.Copy).then_inc(w_vo_ok, 1)
                if b is not None and b >= 1:
                    x1_whole(b - 1)
                if a is not None:
                    query_exp(a)
                if a is not None:
                    act.wait_ge(kx_mm, a + 1)
                    nc.scalar.activation(kx[:, a % 2], small[:], ACT.Copy).then_inc(kx_ok, 1)
                    if a == 0:
                        act.wait_ge(gate_in, 16)
                        nc.scalar.activation(wgate_hi[:, 0:GATES], wgate[:, 0:GATES], ACT.Copy)
                        nc.scalar.activation(wgate_hi[:, GATES:2 * GATES], wgate[:, GATES:2 * GATES], ACT.Copy,
                                             scale=0.5).then_inc(split_hi, 1)
                    act.wait_ge(kxt_mm, a + 1)
                    nc.scalar.activation(kx_t[:, a % 2], small[:, 0:D], ACT.Copy).then_inc(kxt_ok, 1)
                if t is not None:
                    tanh(ps_f, f_mm, t, keep_ok, th_f, 0.5, half_b[:, 0:1] if t else first_b[:, 0:1], f_ok)
                if b is not None:
                    normalise(b, x1[:, b], x1_act_ok, DVE_CHUNKS)
                if t is not None:
                    tanh(ps_i, i_mm, t, new_ok, th_i, 0.5, half_b[:, 1:2] if t else first_b[:, 1:2], i_ok)
                    tanh(ps_c, c_mm, t, new_ok, th_c, 1.0, col[:, BC:BC + 1] if t else first_b[:, 2:3], c_ok)
                if b == T - 1:
                    x1_high(b)
                    x1_whole(b)
            for t in range(T + 3):
                if t < T:
                    act.wait_ge(out_mm, t + 1)
                    if t >= 2:
                        act.wait_ge(w_ok, t - 1)
                        act.wait_ge(wp_ok, t - 1)
                    nc.scalar.activation(h_rows[:, t % 2].rearrange("p c d -> p (c d)"), out_banks[t], ACT.Tanh).then_inc(h_ok, 1)
                if t >= 3:
                    normalise(T + t - 3, x1[:, t - 3], y2_act_ok, 1)

        @block.vector
        def _(dve):
            def setup():
                dve.wait_ge(vec_in, 32)
                nc.vector.memset(bias_z[:], 1.0).then_inc(dve_c, 1)
                nc.vector.memset(eps_z[:], Z_EPS).then_inc(dve_c, 1)
                nc.vector.tensor_scalar(row_t[:, BK_ROW], row[:, BK_ROW], 1.0, None, ALU.add).then_inc(dve_c, 1)
                nc.vector.tensor_copy(row_t[:, BOUT_ROW], row[:, BOUT_ROW]).then_inc(dve_c, 1)
                nc.vector.tensor_scalar(half_b[:], col[:, BF:BI + 1], 0.5, None, ALU.mult).then_inc(dve_c, 1)
                nc.vector.tensor_scalar(s0[:], col[:, C0:C0 + 1], 2.0, None, ALU.mult).then_inc(dve_c, 1)
                dve.wait_ge(dve_c, 4)
                nc.vector.tensor_copy(row_hi[:], row_t[:]).then_inc(dve_c, 1)
                dve.wait_ge(dve_c, 7)
                nc.vector.tensor_tensor(row_lo[:], row_t[:], row_hi[:].bitcast(F32), ALU.subtract).then_inc(dve_c, 1)
                dve.wait_ge(dve_c, 8)
                dve.wait_ge(ident_ok, 1)
                nc.vector.tensor_scalar(row_t[:], row_hi[:].bitcast(F32), ident[:, 0:1], None, ALU.mult).then_inc(dve_c, 1)
                dve.wait_ge(dve_c, 9)
                nc.vector.scalar_tensor_tensor(row_parts[:], row_lo[:].bitcast(F32), ident[:, 1:2], row_t[:],
                                               ALU.mult, ALU.add).then_inc(rows_ok, 1)
                dve.wait_ge(ones_ok, 4)
                nc.vector.tensor_scalar(bv_wide[:], ones_r[:].bitcast(F32), col[:, BV:BV + 1], None,
                                        ALU.mult).then_inc(vecs_ok, 1)
                nc.vector.tensor_scalar(eps_z[:, 0:D], row[:, BATT_ROW], Z_EPS, None, ALU.mult).then_inc(dve_c, 1)

            def setup_products():
                dve.wait_ge(setup_mm, 2)
                nc.vector.tensor_tensor(bias_z[:, 0:D], ps_x1[:, 0:D], row[:, BATT_ROW], ALU.add).then_inc(bias_z_ok, 1)
                dve.wait_ge(setup_mm, 3)
                nc.vector.tensor_tensor(first_b[:], ps_c[:, 0:GATES], col[:, BF:BC + 1], ALU.add).then_inc(first_b_ok, 1)
                dve.wait_ge(first_b_ok, 1)
                nc.vector.tensor_scalar(first_b[:, 0:2], first_b[:, 0:2], 0.5, None, ALU.mult).then_inc(first_b_ok, 1)

            def split_low():
                dve.wait_ge(split_hi, 1)
                nc.vector.tensor_tensor(wgate_lo[:, 0:GATES], wgate[:, 0:GATES], wgate_hi[:, 0:GATES].bitcast(F32),
                                        ALU.subtract)
                g = slice(GATES, 2 * GATES)
                nc.vector.scalar_tensor_tensor(
                    wgate_lo[:, g].rearrange("p g d -> p (g d)"), wgate[:, g].rearrange("p g d -> p (g d)"), 0.5,
                    wgate_hi[:, g].rearrange("p g d -> p (g d)").bitcast(F32), ALU.mult, ALU.subtract).then_inc(split_lo, 1)
                dve.wait_ge(out_in, 16)
                nc.vector.tensor_scalar(uo_half[:], wout[:, 1], 0.5, None, ALU.mult).then_inc(dve_c, 1)

            def statistics(n, tile):
                for c in range(C):
                    st = nc.vector.bn_stats(stats[:, n % 4, c], tile[:, c])
                st.then_inc(st_ok, 1)

            def moments(n):
                dve.wait_ge(st_ok, n + 1)
                for c in range(C):
                    ag = nc.vector.bn_aggr(mean_var[:, n % 4, c], stats[:, n % 4, c])
                ag.then_inc(agg_ok, 1)
                dve.wait_ge(agg_ok, n + 1)
                nc.vector.tensor_scalar(var_eps[:, n % 4], mean_var[:, n % 4, :, 1], LN_EPS, None,
                                        ALU.add).then_inc(var_ok, 1)
                nc.vector.tensor_scalar(neg_mean[:, n % 4], mean_var[:, n % 4, :, 0], -1.0, None,
                                        ALU.mult).then_inc(var_ok, 1)

            def normalise(n, tile, done, chunks):
                dve.wait_ge(rstd_ok, n + 1)
                for c in range(chunks):
                    ins = nc.vector.tensor_scalar(tile[:, c], tile[:, c], mean_var[:, n % 4, c, 0:1],
                                                  rstd[:, n % 4, c:c + 1], ALU.subtract, ALU.mult)
                ins.then_inc(done, 1)

            def residual(b):
                dve.wait_ge(ctx_mm, b + 1)
                nc.vector.reciprocal(z_inv[:, b % 2].rearrange("p (b c) -> p b c", c=2),
                                     ctx_view[:, :, :, D]).then_inc(z_ok, 1)
                dve.wait_ge(z_ok, b + 1)
                for c in range(C):
                    ins = nc.vector.scalar_tensor_tensor(x1[:, b, c], ctx_view[:, c // 2, c % 2, 0:D],
                                                         z_inv[:, b % 2, c:c + 1], x_rows[:, b, c, 0:D], ALU.mult, ALU.add)
                ins.then_inc(y_ok, 1)

            def x1_low(b):
                dve.wait_ge(x1hi_ok, b + 1)
                nc.vector.tensor_tensor(x1_lo[:, b % 2], ps_x1[:], x1_hi[:, b % 2].bitcast(F32),
                                        ALU.subtract).then_inc(x1lo_ok, 1)

            setup()
            for a, b, t in periods():
                if b is not None and b >= 1:
                    x1_low(b - 1)
                if b is not None:
                    residual(b)
                if a is not None:
                    dve.wait_ge(k_exp_ok, a + 1)
                    nc.vector.scalar_tensor_tensor(k_rows[:, a % 2], k_exp[:, a % 2], 1.0,
                                                   ps_k[:].rearrange("p (c d) -> p c d", d=D), ALU.min,
                                                   ALU.max).then_inc(k_ok, 1)
                    if a == 0:
                        setup_products()
                if b is not None:
                    dve.wait_ge(y_ok, b + 1)
                    statistics(b, x1[:, b])
                    moments(b)
                if a is not None:
                    dve.wait_ge(q_exp_ok, a + 1)
                    dve.wait_ge(q_relu_ok, a + 1)
                    nc.vector.scalar_tensor_tensor(q_cols[:, a % 2].rearrange("p c d -> p (c d)"), q_exp[:, a % 2], 1.0,
                                                   q_relu[:, a % 2], ALU.min, ALU.add).then_inc(q_ok, 1)
                    dve.wait_ge(kx_ok, a + 1)
                    if a == 0:
                        dve.wait_ge(bias_z_ok, 1)
                    nc.vector.scalar_tensor_tensor(kvo[:, a % 2], bias_z[:], kx[:, a % 2, D:DZ], eps_z[:],
                                                   ALU.mult, ALU.add).then_inc(kvo_b, 1)
                if b is not None:
                    normalise(b, x1[:, b], x1_ok, DVE_CHUNKS)
                if a is not None:
                    dve.wait_ge(kvo_b, a + 1)
                    dve.wait_ge(kvo_mm, a + 1)
                    nc.vector.tensor_tensor(kvo[:, a % 2, 0:D], kvo[:, a % 2, 0:D], small[:, 0:D],
                                            ALU.add).then_inc(kvo_ok, 1)
                    if a == 0:
                        split_low()
                if t is not None:
                    dve.wait_ge(f_ok, t + 1)
                    if t == 0:
                        nc.vector.tensor_scalar(keep[:], th_f[:], 1.0, s0[:, 0:1], ALU.add, ALU.mult).then_inc(keep_ok, 1)
                    else:
                        nc.vector.scalar_tensor_tensor(keep[:], th_f[:], 1.0, s[:, (t - 1) % 2].rearrange("p c d -> p (c d)"),
                                                       ALU.add, ALU.mult).then_inc(keep_ok, 1)
                    dve.wait_ge(i_ok, t + 1)
                    dve.wait_ge(c_ok, t + 1)
                    nc.vector.scalar_tensor_tensor(new[:], th_i[:], 1.0, th_c[:], ALU.add, ALU.mult).then_inc(new_ok, 1)
                    dve.wait_ge(keep_ok, t + 1)
                    dve.wait_ge(new_ok, t + 1)
                    nc.vector.scalar_tensor_tensor(s[:, t % 2].rearrange("p c d -> p (c d)"), keep[:], 0.5, new[:],
                                                   ALU.mult, ALU.add).then_inc(s_ok, 1)
                if b == T - 1:
                    x1_low(b)
            for t in range(T + 3):
                if t < T:
                    dve.wait_ge(h_ok, t + 1)
                    nc.vector.tensor_tensor(x1[:, t, 0:WC], x1[:, t, 0:WC], h_rows[:, t % 2, 0:WC], ALU.add).then_inc(w_ok, 1)
                if 1 <= t <= T:
                    dve.wait_ge(w_ok, t)
                    dve.wait_ge(wp_ok, t)
                    statistics(T + t - 1, x1[:, t - 1])
                if t >= 3:
                    normalise(T + t - 3, x1[:, t - 3], y2_ok, 1)
                if 1 <= t <= T:
                    moments(T + t - 1)


def kernel(**inputs):
    import numpy as np
    import concourse.bacc as bacc
    from concourse.bass_utils import run_bass_kernel_spmd

    i = {name.removeprefix("L0_"): np.asarray(a) for name, a in inputs.items()}
    x = np.ascontiguousarray(i["attn_x"])
    xt = np.ascontiguousarray(x.reshape(T, D, C, D).transpose(0, 3, 2, 1))

    def packed(*mats):
        return np.ascontiguousarray(np.stack(mats, axis=1))

    arrays = {
        "x": x,
        "xt": xt,
        "w_att": packed(i["attn_Wk"].T, i["attn_Wq"].T, i["attn_Wv"], i["attn_Wo"].T),
        "w_gate": packed(*(i["ffn_" + n].T for n in ("wf", "wi", "wc", "uf", "ui", "uc"))),
        "w_out": packed(i["ffn_wo"].T, i["ffn_uo"].T),
        "cols": packed(i["attn_bq"], i["ffn_bf"], i["ffn_bi"], i["ffn_bc"], i["ffn_in_c"], i["attn_bv"]),
        "rows": np.ascontiguousarray(np.stack([i["attn_bk"], i["ffn_bo"], i["attn_bo"]])),
    }
    nc = bacc.Bacc("TRN2", target_bir_lowering=False, num_devices=1)
    aps = [nc.dram_tensor(n, a.shape, F32, kind="ExternalInput").ap() for n, a in arrays.items()]
    out = nc.dram_tensor("out", (T, N, D), F32, kind="ExternalOutput").ap()
    build(nc, *aps, out)
    return run_bass_kernel_spmd(nc, [arrays], core_ids=[0]).results[0]["out"]
```

```python
from contextlib import ExitStack

import concourse.bass as bass
from concourse import mybir

ALU = mybir.AluOpType
ACT = mybir.ActivationFunctionType
F32 = mybir.dt.float32
F32R = mybir.dt.float32r

T = 8
N = 512
D = 128
C = N // D
DZ = D + 1
H_TILES = 4
DVE_AHEAD, POOL_AHEAD, ACT_AHEAD = 2, 3, 4
WC = 2
UNITS = [(t, 0, C) for t in range(T - 1)] + [(T - 1, 0, C // 2), (T - 1, C // 2, C)]
DVE_NORM = [0, 1, 0, 1, 0, 0, 3, 2, 2]
LN_EPS = 1e-5
Z_EPS = 1e-6

WK_T, WQ_T = range(2)
WV, WO_T = range(2)
GATES = 3
BQ, BF, BI, BC, C0, BV = range(6)
COLS = 6
BK_ROW, BOUT_ROW = range(2)
HIGH, LOW, ONE = 0, 32, 64
WARM_UP = 8


def build(nc, x, xt, w_kq, w_vo_in, w_gate, w_out, rows, att_row, out):
    with ExitStack() as ctx:
        def sb(name, shape, dt=F32):
            return ctx.enter_context(nc.sbuf_tensor(name, shape, dt))

        def bank(name):
            return ctx.enter_context(nc.psum_tensor(name, [D, N], F32))

        def sem(name):
            return ctx.enter_context(nc.semaphore(name))

        x_rows = sb("x_rows", [D, T, C, D])
        x_cols = sb("x_cols", [D, T, C, D])
        wkq = sb("wkq", [D, 2 * D + COLS])
        wvo_in = sb("wvo_in", [D, 2, D])
        wgate = sb("wgate", [D, 2 * GATES, D])
        wout = sb("wout", [D, 2, D])
        col = wkq[:, 2 * D:]
        row = sb("row", [LOW + 1, 2, D])
        batt = sb("batt", [D, D])

        ident = sb("ident", [D, D])
        ones_r = sb("ones_r", [D, D], F32R)
        minus_half = sb("minus_half", [D, C])
        minus_one = sb("minus_one", [D, 1])
        half_b = sb("half_b", [D, 2])
        s0 = sb("s0", [D, 1])
        first_b = sb("first_b", [D, GATES])
        wgate_hi = sb("wgate_hi", [D, 2 * GATES, D], F32R)
        wgate_lo = sb("wgate_lo", [D, 2 * GATES, D], F32R)
        uo_half = sb("uo_half", [D, D])
        bv_wide = sb("bv_wide", [D, D])
        w_vo = sb("w_vo", [D, D])
        bias_z = sb("bias_z", [D, DZ])
        eps_z = sb("eps_z", [D, DZ])
        row_hi = sb("row_hi", [LOW + 1, 2, D], F32R)
        row_parts = sb("row_parts", [D, 2, D], F32R)
        table = sb("table", [D, 1])

        k_exp = sb("k_exp", [D, 2, C, D])
        k_rows = sb("k_rows", [D, 2, C, D])
        q_exp = sb("q_exp", [D, 2, N])
        q_relu = sb("q_relu", [D, 2, N])
        q_cols = sb("q_cols", [D, 2, C, D])
        k_pair = sb("k_pair", [D, 2, D])
        k_sum = sb("k_sum", [D, 2, D])
        xk = sb("xk", [D, 2, D])
        kvo = sb("kvo", [D, 2, DZ])
        z_inv = sb("z_inv", [D, 2, C])
        x1 = sb("x1", [D, T, C, D])
        stats = sb("stats", [D, 2 * T, C, 6])
        mean_var = sb("mean_var", [D, 2 * T, C, 2])
        var_eps = sb("var_eps", [D, 2 * T, C])
        rstd = sb("rstd", [D, 2 * T, C])
        shift = sb("shift", [D, T, C])
        x1_cols = sb("x1_cols", [D, T, C, D])
        x1_hi = sb("x1_hi", [D, 2, N], F32R)
        x1_lo = sb("x1_lo", [D, 2, N], F32R)
        th_f = sb("th_f", [D, N])
        th_i = sb("th_i", [D, N])
        th_c = sb("th_c", [D, N])
        keep = sb("keep", [D, N])
        new = sb("new", [D, N])
        s = sb("s", [D, 2, C, D])
        s_hi = sb("s_hi", [D, 2, N], F32R)
        s_lo = sb("s_lo", [D, 2, N], F32R)
        h_rows = sb("h_rows", [D, H_TILES, C, D])

        ps_k, ps_q = bank("ps_k"), bank("ps_q")
        ps_f, ps_i, ps_c = bank("ps_f"), bank("ps_i"), bank("ps_c")
        ps_x1 = bank("ps_x1")
        ps_ctx = ctx.enter_context(nc.psum_tensor("ps_ctx", [D, 2, N], F32))
        ctx_view = ps_ctx[:, :, 0:2 * DZ].rearrange("p b (c d) -> p b c d", d=DZ)
        small = ps_ctx[:, 1, 2 * DZ:3 * DZ]
        out_banks = [ps_k[:], ps_q[:], ps_ctx[:, 0, :], ps_ctx[:, 1, :], ps_x1[:], ps_f[:], ps_i[:], ps_c[:]]
        OUT_PARTS = [(0, 0, C // 2, out_banks[0]), (0, C // 2, C, out_banks[5])]
        OUT_PARTS += [(t, 0, C, out_banks[t]) for t in range(1, T)]

        kq_in, vo_in, gate_in, out_in = sem("kq_in"), sem("vo_in"), sem("gate_in"), sem("out_in")
        row_in, batt_in = sem("row_in"), sem("batt_in")
        x_rows_in = [sem(f"x_rows_in{t}") for t in range(T)]
        x_cols_in = [sem(f"x_cols_in{t}") for t in range(T)]
        ident_ok, ones_ok, minus_one_ok, pool_c = sem("ident_ok"), sem("ones_ok"), sem("minus_one_ok"), sem("pool_c")
        vecs_ok, rows_ok, eps_z_ok, dve_c = sem("vecs_ok"), sem("rows_ok"), sem("eps_z_ok"), sem("dve_c")
        s0_ok, halved_ok, uo_ok = sem("s0_ok"), sem("halved_ok"), sem("uo_ok")
        split_hi, split_lo, split_s_lo = sem("split_hi"), sem("split_lo"), sem("split_s_lo")
        setup_mm, bias_z_ok, w_vo_ok, first_b_ok = sem("setup_mm"), sem("bias_z_ok"), sem("w_vo_ok"), sem("first_b_ok")
        k_mm, k_exp_ok, k_ok = sem("k_mm"), sem("k_exp_ok"), sem("k_ok")
        q_mm, q_exp_ok, q_relu_ok, q_ok = sem("q_mm"), sem("q_exp_ok"), sem("q_relu_ok"), sem("q_ok")
        k_pair_ok, k_sum_ok, xk_mm, xk_ok = sem("k_pair_ok"), sem("k_sum_ok"), sem("xk_mm"), sem("xk_ok")
        kvo_mm, kvo_ok = sem("kvo_mm"), sem("kvo_ok")
        ctx_mm, z_ok, y_ok = sem("ctx_mm"), sem("z_ok"), sem("y_ok")
        y_small_ok = sem("y_small_ok")
        st_ok, agg_ok, var_ok, rstd_ok, x1_ok = sem("st_ok"), sem("agg_ok"), sem("var_ok"), sem("rstd_ok"), sem("x1_ok")
        shift_ok = sem("shift_ok")
        x1t_mm, x1c_ok, x1hi_ok, x1lo_ok = sem("x1t_mm"), sem("x1c_ok"), sem("x1hi_ok"), sem("x1lo_ok")
        f_mm, i_mm, c_mm = sem("f_mm"), sem("i_mm"), sem("c_mm")
        f_ok, i_ok, c_ok = sem("f_ok"), sem("i_ok"), sem("c_ok")
        keep_ok, new_ok, s_ok, shi_ok, slo_ok = sem("keep_ok"), sem("new_ok"), sem("s_ok"), sem("shi_ok"), sem("slo_ok")
        out_mm, h_ok, w_ok, y2_ok, stored = sem("out_mm"), sem("h_ok"), sem("w_ok"), sem("y2_ok"), sem("stored")
        y2_act_ok, wp_ok = sem("y2_act_ok"), sem("wp_ok")

        block = ctx.enter_context(nc.Block())

        def rows_of(dram, t):
            return dram[t].rearrange("(p c) d -> p c d", c=C)

        def halves(cut):
            return [slice(0, N // 2), slice(N // 2, N)] if cut else [slice(0, N)]

        def act_norms(units):
            return sum(c1 - c0 - mine for (_, c0, c1), mine in zip(UNITS[:units], DVE_NORM))

        def periods():
            def inside(v):
                return v if 0 <= v < T else None
            for n in range(T + 2):
                yield inside(n + 1), inside(n), inside(n - 1), inside(n - 2)

        @block.sync
        def _(sp):
            sp.dma_start(x_cols[:, 0], xt[0]).then_inc(x_cols_in[0], 16)
            sp.dma_start(row[:], rows.partition_broadcast(LOW + 1)).then_inc(row_in, 16)
            sp.dma_start(wvo_in[:], w_vo_in).then_inc(vo_in, 16)
            sp.dma_start(x_rows[:, 0], rows_of(x, 0)).then_inc(x_rows_in[0], 16)
            sp.dma_start(batt[:], att_row.partition_broadcast(D)).then_inc(batt_in, 16)
            sp.dma_start(wgate[:], w_gate).then_inc(gate_in, 16)
            for t in range(1, T):
                sp.dma_start(x_cols[:, t], xt[t]).then_inc(x_cols_in[t], 16)
                sp.dma_start(x_rows[:, t], rows_of(x, t)).then_inc(x_rows_in[t], 16)
                if t == 1:
                    sp.dma_start(wout[:], w_out).then_inc(out_in, 16)
            for u, (t, c0, c1) in enumerate(UNITS):
                sp.wait_ge(y2_ok, sum(DVE_NORM[:u + 1]))
                sp.wait_ge(y2_act_ok, act_norms(u + 1))
                sp.dma_start(rows_of(out, t)[:, c0:c1], x1[:, t, c0:c1]).then_inc(stored, 16)
            sp.wait_ge(stored, 16 * len(UNITS))

        @block.gpsimd
        def _(pool):
            nc.gpsimd.memset(minus_one[:], -1.0).then_inc(minus_one_ok, 1)
            nc.gpsimd.memset(ident[:], 0.0).then_inc(pool_c, 1)
            nc.gpsimd.memset(minus_half[:], -0.5).then_inc(pool_c, 1)
            pool.wait_ge(pool_c, 2)
            nc.gpsimd.affine_select(out=ident[:], in_=ident[:], compare_op=ALU.not_equal, fill=1.0, base=0,
                                    pattern=[[-1, D]], channel_multiplier=1).then_inc(ident_ok, 1)

            def key_sums(a):
                pool.wait_ge(k_ok, a + 1)
                if a >= 1:
                    pool.wait_ge(k_sum_ok, a)
                nc.gpsimd.tensor_tensor(k_pair[:], k_rows[:, a % 2, 0:C // 2], k_rows[:, a % 2, C // 2:C],
                                        ALU.add).then_inc(k_pair_ok, 1)
                pool.wait_ge(k_pair_ok, a + 1)
                if a >= 2:
                    pool.wait_ge(kvo_mm, a - 1)
                nc.gpsimd.tensor_tensor(k_sum[:, a % 2], k_pair[:, 0], k_pair[:, 1], ALU.add).then_inc(k_sum_ok, 1)

            def reciprocal_root(n, t, c0=0, c1=C):
                pool.wait_ge(var_ok, n + 1)
                nc.gpsimd.tensor_tensor(rstd[:, t, c0:c1], var_eps[:, t, c0:c1], minus_half[:, c0:c1],
                                        ALU.pow).then_inc(rstd_ok, 1)

            def second_residual(t):
                pool.wait_ge(h_ok, t + 2)
                nc.gpsimd.tensor_tensor(x1[:, t, WC:], x1[:, t, WC:], h_rows[:, t % H_TILES, WC:], ALU.add).then_inc(wp_ok, 1)

            def halve_weights():
                pool.wait_ge(gate_in, 16)
                nc.gpsimd.tensor_scalar(wgate[:, GATES:], wgate[:, GATES:], 0.5, None, ALU.mult).then_inc(halved_ok, 1)

            def split_state_low():
                pool.wait_ge(split_hi, 2)
                nc.gpsimd.tensor_tensor(wgate_lo[:, GATES:], wgate[:, GATES:], wgate_hi[:, GATES:].bitcast(F32),
                                        ALU.subtract).then_inc(split_s_lo, 1)
                pool.wait_ge(out_in, 16)
                nc.gpsimd.tensor_scalar(uo_half[:], wout[:, 1], 0.5, None, ALU.mult).then_inc(uo_ok, 1)

            key_sums(0)
            for k, a, b, t in periods():
                if t is not None and 1 <= t < T - 1:
                    pool.wait_ge(shi_ok, t)
                    nc.gpsimd.tensor_tensor(s_lo[:, (t - 1) % 2], s[:, (t - 1) % 2].rearrange("p c d -> p (c d)"),
                                            s_hi[:, (t - 1) % 2].bitcast(F32), ALU.subtract).then_inc(slo_ok, 1)
                if b is not None:
                    reciprocal_root(b, b)
                if k is not None:
                    key_sums(k)
                if a == 0:
                    halve_weights()
                if a == 1:
                    split_state_low()
            for t in range(1, POOL_AHEAD):
                second_residual(t)
            for u, (t, c0, c1) in enumerate(UNITS):
                reciprocal_root(T + u, T + t, c0, c1)
                if t + POOL_AHEAD < T:
                    second_residual(t + POOL_AHEAD)

        @block.tensor
        def _(pe):
            def warm_up():
                pe.wait_ge(ones_ok, 1)
                for _ in range(WARM_UP):
                    nc.tensor.matmul(ps_f[:], ones_r[:], ones_r[:].unsqueeze(1).to_broadcast([D, C, D]),
                                     start=True, stop=True)

            def keys(a):
                if a == 0:
                    pe.wait_ge(kq_in, 16)
                pe.wait_ge(x_cols_in[a], 16)
                if a >= 1:
                    pe.wait_ge(k_exp_ok, a)
                    pe.wait_ge(k_ok, a)
                for c in range(C):
                    nc.tensor.matmul(ps_k[:, c * D:(c + 1) * D], x_cols[:, a, c], wkq[:, WK_T * D:(WK_T + 1) * D],
                                     start=(c == 0), stop=False, skip_group_check=True)
                if a == 0:
                    pe.wait_ge(rows_ok, 1)
                nc.tensor.matmul(ps_k[:], ones_r[:], row_parts[:, BK_ROW].unsqueeze(1).to_broadcast([D, C, D]),
                                 start=False, stop=True, skip_group_check=True).then_inc(k_mm, 1)

            def queries(a):
                if a >= 1:
                    pe.wait_ge(q_relu_ok, a)
                nc.tensor.matmul(ps_q[:], wkq[:, WQ_T * D:(WQ_T + 1) * D], x_cols[:, a].rearrange("p c d -> p (c d)"),
                                 start=True, stop=True).then_inc(q_mm, 1)

            def keys_x(a):
                pe.wait_ge(x_rows_in[a], 16)
                pe.wait_ge(k_ok, a + 1)
                if a >= 1:
                    pe.wait_ge(y_small_ok, a)
                for c in range(C):
                    mm = nc.tensor.matmul(small[:, 0:D], x_rows[:, a, c], k_rows[:, a % 2, c],
                                          start=(c == 0), stop=(c == C - 1))
                mm.then_inc(xk_mm, 1)

            def key_values(a):
                if a == 0:
                    pe.wait_ge(bias_z_ok, 1)
                    pe.wait_ge(w_vo_ok, 1)
                pe.wait_ge(k_sum_ok, a + 1)
                pe.wait_ge(xk_ok, a + 1)
                nc.tensor.matmul(small[:], k_sum[:, a % 2], bias_z[:], start=True, stop=False, skip_group_check=True)
                nc.tensor.matmul(small[:, 0:D], xk[:, a % 2], w_vo[:], start=False, stop=True,
                                 skip_group_check=True).then_inc(kvo_mm, 1)

            def context(b):
                pe.wait_ge(q_ok, b + 1)
                pe.wait_ge(kvo_ok, b + 1)
                if b >= 1:
                    pe.wait_ge(y_ok, b)
                for c in range(C):
                    mm = nc.tensor.matmul(ctx_view[:, c // 2, c % 2], q_cols[:, b % 2, c], kvo[:, b % 2],
                                          start=True, stop=True, skip_group_check=True)
                mm.then_inc(ctx_mm, 1)

            def x1_turned(b):
                if b == 0:
                    pe.wait_ge(ident_ok, 1)
                if b >= 1:
                    pe.wait_ge(x1c_ok, b)
                for c in range(C):
                    pe.wait_ge(x1_ok, b * C + c + 1)
                    mm = nc.tensor.transpose(ps_x1[:, c * D:(c + 1) * D], x1[:, b, c], ident[:])
                mm.then_inc(x1t_mm, 1)

            gates = [(ps_f, f_ok, f_mm), (ps_i, i_ok, i_mm), (ps_c, c_ok, c_mm)]

            def gate_x_high(g, t):
                ps, used, _ = gates[g]
                if t == 0:
                    pe.wait_ge(split_lo, 1)
                if t >= 1:
                    pe.wait_ge(used, t)
                pe.wait_ge(x1hi_ok, t + 1)
                nc.tensor.matmul(ps[:], wgate_hi[:, g], x1_hi[:, t % 2], start=True, stop=False)
                nc.tensor.matmul(ps[:], wgate_lo[:, g], x1_hi[:, t % 2], start=False, stop=False)

            def gate_x_low(g, t):
                ps, _, done = gates[g]
                pe.wait_ge(x1lo_ok, t + 1)
                mm = nc.tensor.matmul(ps[:], wgate_hi[:, g], x1_lo[:, t % 2], start=False, stop=(t == 0))
                if t == 0:
                    mm.then_inc(done, 1)

            def gate_s_high(g, t):
                ps, u, last = gates[g][0], GATES + g, (t - 1) % 2
                if t == 1:
                    pe.wait_ge(split_s_lo, 1)
                pe.wait_ge(shi_ok, t)
                nc.tensor.matmul(ps[:], wgate_hi[:, u], s_hi[:, last], start=False, stop=False)
                nc.tensor.matmul(ps[:], wgate_lo[:, u], s_hi[:, last], start=False, stop=False)

            def gate_s_low(g, t):
                ps, _, done = gates[g]
                pe.wait_ge(slo_ok, t)
                nc.tensor.matmul(ps[:], wgate_hi[:, GATES + g], s_lo[:, (t - 1) % 2], start=False, stop=True).then_inc(done, 1)

            def gate_s(g, t):
                gate_s_high(g, t)
                gate_s_low(g, t)

            def out_x(o):
                t, c0, c1, ps = OUT_PARTS[o]
                if o == 0:
                    pe.wait_ge(out_in, 16)
                    pe.wait_ge(k_ok, T)
                    pe.wait_ge(x1c_ok, 1)
                if o == 1:
                    pe.wait_ge(f_ok, T)
                if t == 1:
                    pe.wait_ge(x1c_ok, 2)
                    pe.wait_ge(q_relu_ok, T)
                if t == 2:
                    pe.wait_ge(x1c_ok, 3)
                    pe.wait_ge(y_ok, T)
                    pe.wait_ge(y_small_ok, T)
                if t == 4:
                    pe.wait_ge(x1c_ok, T)
                if t == 5:
                    pe.wait_ge(h_ok, 2)
                if t == 6:
                    pe.wait_ge(i_ok, T)
                if t == 7:
                    pe.wait_ge(c_ok, T + 1)
                for c in range(c0, c1):
                    nc.tensor.matmul(ps[:, c * D:(c + 1) * D], x1_cols[:, t, c], wout[:, 0],
                                     start=(c == c0), stop=False, skip_group_check=True)
                nc.tensor.matmul(ps[:, c0 * D:c1 * D], ones_r[:],
                                 row_parts[:, BOUT_ROW].unsqueeze(1).to_broadcast([D, c1 - c0, D]),
                                 start=False, stop=False, skip_group_check=True)

            def out_s(o):
                _, c0, c1, ps = OUT_PARTS[o]
                if o == 0:
                    pe.wait_ge(uo_ok, 1)
                if o < 2:
                    pe.wait_ge(s_ok, T + o)
                for c in range(c0, c1):
                    mm = nc.tensor.matmul(ps[:, c * D:(c + 1) * D], s[:, (T - 1) % 2, c], uo_half[:],
                                          start=False, stop=(c == c1 - 1), skip_group_check=True)
                mm.then_inc(out_mm, 1)

            def setup_attention():
                pe.wait_ge(vo_in, 16)
                nc.tensor.matmul(ps_i[:, 0:D], wvo_in[:, WV], wvo_in[:, WO_T], start=True, stop=True,
                                 skip_group_check=True).then_inc(setup_mm, 1)
                pe.wait_ge(vecs_ok, 1)
                nc.tensor.matmul(ps_x1[:, 0:D], bv_wide[:], wvo_in[:, WO_T], start=True, stop=True,
                                 skip_group_check=True).then_inc(setup_mm, 1)

            def setup_gates():
                pe.wait_ge(halved_ok, 1)
                pe.wait_ge(s0_ok, 1)
                for g in range(GATES):
                    mm = nc.tensor.matmul(ps_c[:, g:g + 1], wgate[:, GATES + g], s0[:],
                                          start=True, stop=True, skip_group_check=True)
                mm.then_inc(setup_mm, 1)

            warm_up()
            keys(0)
            queries(0)
            setup_attention()
            for k, a, b, t in periods():
                if a == 0:
                    keys_x(a)
                    keys(k)
                    key_values(a)
                    queries(k)
                    context(a)
                    continue
                if k is not None:
                    keys(k)
                    if a == 1:
                        keys_x(a)
                    if a in (2, 3):
                        x1_turned(a - 2)
                    queries(k)
                if a == T - 1:
                    out_x(0)
                if t == T - 2:
                    out_x(2)
                if t == 0:
                    gate_x_high(0, t)
                    keys_x(a)
                    gate_x_low(0, t)
                    gate_x_high(1, t)
                    key_values(a)
                    gate_x_low(1, t)
                    gate_x_high(2, t)
                    gate_x_low(2, t)
                    context(a)
                    continue
                if t is not None:
                    for g in range(GATES):
                        gate_x_high(g, t)
                    for g in range(GATES):
                        gate_x_low(g, t)
                    if a is not None:
                        keys_x(a)
                    gate_s(0, t)
                if a is not None:
                    key_values(a)
                if a == 1:
                    setup_gates()
                if t is not None:
                    gate_s(1, t)
                    gate_s(2, t)
                if a is not None:
                    context(a)
                if t == T - 2:
                    out_x(3)
                if b is not None and b >= 2:
                    x1_turned(b)
                if b == T - 1:
                    out_x(4)
            out_x(1)
            out_x(5)
            for o in range(len(OUT_PARTS)):
                if o >= 6:
                    out_x(o)
                out_s(o)

        @block.scalar
        def _(act):
            act.dma_start(wkq[:], w_kq).then_inc(kq_in, 16)
            act.wait_ge(minus_one_ok, 1)
            nc.scalar.activation(table[:], minus_one[:], ACT.Exp)

            def key_exp(a):
                act.wait_ge(k_mm, a + 1)
                nc.scalar.activation(k_exp[:, a % 2].rearrange("p c d -> p (c d)"), ps_k[:], ACT.Exp,
                                     bias=minus_one[:, 0:1]).then_inc(k_exp_ok, 1)

            def query_exp(a):
                act.wait_ge(q_mm, a + 1)
                nc.scalar.activation(q_exp[:, a % 2], ps_q[:], ACT.Exp, bias=col[:, BQ:BQ + 1]).then_inc(q_exp_ok, 1)
                nc.scalar.activation(q_relu[:, a % 2], ps_q[:], ACT.Relu, bias=col[:, BQ:BQ + 1]).then_inc(q_relu_ok, 1)

            def tanh(ps, done, t, made, out_tile, scale, bias, ok):
                act.wait_ge(done, t + 1)
                if t >= 1:
                    act.wait_ge(made, t)
                for part in halves(t == T - 1 and ps is ps_c):
                    nc.scalar.activation(out_tile[:, part], ps[:, part], ACT.Tanh, bias=bias, scale=scale).then_inc(ok, 1)

            def normalise(u):
                t, c0, c1 = UNITS[u]
                for c in range(c0 + DVE_NORM[u], c1):
                    act.wait_ge(shift_ok, u + 1)
                    nc.scalar.activation(x1[:, t, c], x1[:, t, c], ACT.Identity, bias=shift[:, t, c:c + 1],
                                         scale=rstd[:, T + t, c:c + 1]).then_inc(y2_act_ok, 1)

            def xk_copy(a):
                act.wait_ge(xk_mm, a + 1)
                nc.scalar.activation(xk[:, a % 2], small[:, 0:D], ACT.Copy).then_inc(xk_ok, 1)

            def x1_high(b):
                act.wait_ge(x1t_mm, b + 1)
                nc.scalar.activation(x1_hi[:, b % 2], ps_x1[:], ACT.Copy).then_inc(x1hi_ok, 1)

            def x1_whole(b):
                act.wait_ge(x1lo_ok, b + 1)
                nc.scalar.activation(x1_cols[:, b].rearrange("p c d -> p (c d)"), ps_x1[:],
                                     ACT.Copy).then_inc(x1c_ok, 1)

            act.wait_ge(kq_in, 16)
            key_exp(0)
            query_exp(0)
            act.wait_ge(setup_mm, 1)
            nc.scalar.activation(w_vo[:], ps_i[:, 0:D], ACT.Copy).then_inc(w_vo_ok, 1)
            for k, a, b, t in periods():
                if a == 0:
                    xk_copy(a)
                if k is not None:
                    key_exp(k)
                if a == 1:
                    xk_copy(a)
                    act.wait_ge(halved_ok, 1)
                    nc.scalar.activation(wgate_hi[:, GATES:2 * GATES], wgate[:, GATES:2 * GATES],
                                         ACT.Copy).then_inc(split_hi, 1)
                if t is not None and t >= 1:
                    act.wait_ge(s_ok, t)
                    nc.scalar.activation(s_hi[:, (t - 1) % 2], s[:, (t - 1) % 2].rearrange("p c d -> p (c d)"),
                                         ACT.Copy).then_inc(shi_ok, 1)
                if t is not None:
                    x1_whole(t)
                if a == 2:
                    xk_copy(a)
                if k is not None:
                    query_exp(k)
                if a == 0:
                    act.wait_ge(gate_in, 16)
                    nc.scalar.activation(wgate_hi[:, 0:GATES], wgate[:, 0:GATES], ACT.Copy).then_inc(split_hi, 1)
                if a is not None and a > 2:
                    xk_copy(a)
                if t is not None:
                    tanh(ps_f, f_mm, t, keep_ok, th_f, 0.5, half_b[:, 0:1] if t else first_b[:, 0:1], f_ok)
                    tanh(ps_i, i_mm, t, new_ok, th_i, 0.5, half_b[:, 1:2] if t else first_b[:, 1:2], i_ok)
                    tanh(ps_c, c_mm, t, new_ok, th_c, 1.0, col[:, BC:BC + 1] if t else first_b[:, 2:3], c_ok)
                if b is not None:
                    x1_high(b)
            for t in range(len(UNITS) + ACT_AHEAD):
                if t < T:
                    if t >= H_TILES:
                        act.wait_ge(w_ok, t - H_TILES + 1)
                        if t > H_TILES:
                            act.wait_ge(wp_ok, t - H_TILES)
                    for o, (_, c0, c1, ps) in enumerate(OUT_PARTS):
                        if OUT_PARTS[o][0] == t:
                            act.wait_ge(out_mm, o + 1)
                            nc.scalar.activation(h_rows[:, t % H_TILES, c0:c1].rearrange("p c d -> p (c d)"),
                                                 ps[:, c0 * D:c1 * D], ACT.Tanh).then_inc(h_ok, 1)
                if t >= ACT_AHEAD:
                    normalise(t - ACT_AHEAD)

        @block.vector
        def _(dve):
            def setup():
                nc.vector.memset(ones_r[:].bitcast(F32), 1.0).then_inc(ones_ok, 1)
                nc.vector.memset(row_parts[:].bitcast(F32), 0.0).then_inc(dve_c, 1)
                nc.vector.memset(bias_z[:], 1.0).then_inc(dve_c, 1)
                nc.vector.memset(eps_z[:], Z_EPS).then_inc(dve_c, 1)
                dve.wait_ge(dve_c, 3)
                nc.vector.memset(row_parts[ONE:ONE + 1, BK_ROW].bitcast(F32), 1.0).then_inc(dve_c, 1)
                dve.wait_ge(dve_c, 4)
                dve.wait_ge(row_in, 16)
                nc.vector.tensor_copy(row_hi[LOW:LOW + 1], row[LOW:LOW + 1]).then_inc(dve_c, 1)
                nc.vector.tensor_copy(row_parts[HIGH:HIGH + 1], row[HIGH:HIGH + 1]).then_inc(dve_c, 1)
                dve.wait_ge(dve_c, 6)
                nc.vector.tensor_tensor(row_parts[LOW:LOW + 1], row[LOW:LOW + 1], row_hi[LOW:LOW + 1].bitcast(F32),
                                        ALU.subtract).then_inc(rows_ok, 1)
                dve.wait_ge(kq_in, 16)
                dve.wait_ge(ones_ok, 1)
                nc.vector.tensor_scalar(bv_wide[:], ones_r[:].bitcast(F32), col[:, BV:BV + 1], None,
                                        ALU.mult).then_inc(vecs_ok, 1)
                nc.vector.tensor_scalar(half_b[:], col[:, BF:BI + 1], 0.5, None, ALU.mult).then_inc(dve_c, 1)
                nc.vector.tensor_scalar(s0[:], col[:, C0:C0 + 1], 2.0, None, ALU.mult).then_inc(s0_ok, 1)
                dve.wait_ge(batt_in, 16)
                nc.vector.tensor_scalar(eps_z[:, 0:D], batt[:], Z_EPS, None, ALU.mult).then_inc(eps_z_ok, 1)

            def setup_products():
                dve.wait_ge(setup_mm, 2)
                nc.vector.tensor_tensor(bias_z[:, 0:D], ps_x1[:, 0:D], batt[:], ALU.add).then_inc(bias_z_ok, 1)

            def first_biases():
                dve.wait_ge(setup_mm, 3)
                nc.vector.tensor_tensor(first_b[:], ps_c[:, 0:GATES], col[:, BF:BC + 1], ALU.add).then_inc(first_b_ok, 1)
                dve.wait_ge(first_b_ok, 1)
                nc.vector.tensor_scalar(first_b[:, 0:2], first_b[:, 0:2], 0.5, None, ALU.mult).then_inc(first_b_ok, 1)

            def split_low():
                dve.wait_ge(split_hi, 1)
                nc.vector.tensor_tensor(wgate_lo[:, 0:GATES], wgate[:, 0:GATES], wgate_hi[:, 0:GATES].bitcast(F32),
                                        ALU.subtract).then_inc(split_lo, 1)

            def statistics(n, t, tile, c0=0, c1=C):
                for c in range(c0, c1):
                    st = nc.vector.bn_stats(stats[:, t, c], tile[:, c])
                st.then_inc(st_ok, 1)

            def moments(n, t, c0=0, c1=C):
                dve.wait_ge(st_ok, n + 1)
                for c in range(c0, c1):
                    ag = nc.vector.bn_aggr(mean_var[:, t, c], stats[:, t, c])
                ag.then_inc(agg_ok, 1)

            def variance(n, t, c0=0, c1=C):
                dve.wait_ge(agg_ok, n + 1)
                nc.vector.tensor_scalar(var_eps[:, t, c0:c1], mean_var[:, t, c0:c1, 1], LN_EPS, None,
                                        ALU.add).then_inc(var_ok, 1)

            def normalise(b):
                dve.wait_ge(rstd_ok, b + 1)
                for c in range(C):
                    nc.vector.tensor_scalar(x1[:, b, c], x1[:, b, c], mean_var[:, b, c, 0:1], rstd[:, b, c:c + 1],
                                            ALU.subtract, ALU.mult).then_inc(x1_ok, 1)

            def reciprocal_z(b):
                dve.wait_ge(ctx_mm, b + 1)
                nc.vector.reciprocal(z_inv[:, b % 2].rearrange("p (b c) -> p b c", c=2),
                                     ctx_view[:, :, :, D]).then_inc(z_ok, 1)

            def residual(b, chunks, done):
                dve.wait_ge(z_ok, b + 1)
                for c in chunks:
                    ins = nc.vector.scalar_tensor_tensor(x1[:, b, c], ctx_view[:, c // 2, c % 2, 0:D],
                                                         z_inv[:, b % 2, c:c + 1], x_rows[:, b, c, 0:D], ALU.mult, ALU.add)
                ins.then_inc(done, 1)

            def x1_low(b):
                dve.wait_ge(x1hi_ok, b + 1)
                nc.vector.tensor_tensor(x1_lo[:, b % 2], ps_x1[:], x1_hi[:, b % 2].bitcast(F32),
                                        ALU.subtract).then_inc(x1lo_ok, 1)

            def key_max(a):
                dve.wait_ge(k_exp_ok, a + 1)
                nc.vector.scalar_tensor_tensor(k_rows[:, a % 2], k_exp[:, a % 2], 1.0,
                                               ps_k[:].rearrange("p (c d) -> p c d", d=D), ALU.min,
                                               ALU.max).then_inc(k_ok, 1)

            def kept_state(t):
                dve.wait_ge(f_ok, t + 1)
                if t == 0:
                    nc.vector.tensor_scalar(keep[:], th_f[:], 1.0, s0[:, 0:1], ALU.add, ALU.mult).then_inc(keep_ok, 1)
                else:
                    nc.vector.scalar_tensor_tensor(keep[:], th_f[:], 1.0, s[:, (t - 1) % 2].rearrange("p c d -> p (c d)"),
                                                   ALU.add, ALU.mult).then_inc(keep_ok, 1)

            def query_sum(a):
                dve.wait_ge(q_exp_ok, a + 1)
                dve.wait_ge(q_relu_ok, a + 1)
                nc.vector.scalar_tensor_tensor(q_cols[:, a % 2].rearrange("p c d -> p (c d)"), q_exp[:, a % 2], 1.0,
                                               q_relu[:, a % 2], ALU.min, ALU.add).then_inc(q_ok, 1)

            def key_values(a):
                if a == 0:
                    dve.wait_ge(eps_z_ok, 1)
                dve.wait_ge(kvo_mm, a + 1)
                nc.vector.tensor_tensor(kvo[:, a % 2], small[:], eps_z[:], ALU.add).then_inc(kvo_ok, 1)

            setup()
            key_max(0)
            setup_products()
            query_sum(0)
            for k, a, b, t in periods():
                if a == 0:
                    key_values(a)
                    key_max(k)
                    continue
                if t == T - 1:
                    dve.wait_ge(shi_ok, t)
                    nc.vector.tensor_tensor(s_lo[:, (t - 1) % 2], s[:, (t - 1) % 2].rearrange("p c d -> p (c d)"),
                                            s_hi[:, (t - 1) % 2].bitcast(F32), ALU.subtract).then_inc(slo_ok, 1)
                if b is not None:
                    if b < 2:
                        reciprocal_z(b)
                    residual(b, range(C // 2, C), y_small_ok)
                    if b == 1:
                        x1_low(0)
                    residual(b, range(C // 2), y_ok)
                    dve.wait_ge(y_ok, b + 1)
                    dve.wait_ge(y_small_ok, b + 1)
                    statistics(b, b, x1[:, b])
                    moments(b, b)
                    variance(b, b)
                if a == 1:
                    query_sum(a)
                if a in (1, 2):
                    key_values(a)
                if k is not None:
                    key_max(k)
                    if a > 1:
                        query_sum(k)
                if a is not None and a > 2:
                    key_values(a)
                if t == T - 2:
                    kept_state(t)
                if b is not None:
                    normalise(b)
                if a == 1:
                    split_low()
                    first_biases()
                    query_sum(k)
                if t is not None:
                    if t != T - 2:
                        kept_state(t)
                    dve.wait_ge(i_ok, t + 1)
                    parts = halves(t == T - 1)
                    for h, part in enumerate(parts):
                        dve.wait_ge(c_ok, t + 1 + h)
                        nc.vector.scalar_tensor_tensor(new[:, part], th_i[:, part], 1.0, th_c[:, part],
                                                       ALU.add, ALU.mult).then_inc(new_ok, 1)
                    if a is not None:
                        reciprocal_z(a)
                    dve.wait_ge(keep_ok, t + 1)
                    for h, part in enumerate(parts):
                        dve.wait_ge(new_ok, t + 1 + h)
                        nc.vector.scalar_tensor_tensor(s[:, t % 2].rearrange("p c d -> p (c d)")[:, part], keep[:, part], 0.5,
                                                       new[:, part], ALU.mult, ALU.add).then_inc(s_ok, 1)
                if b is not None and b >= 1:
                    x1_low(b)

            def second_residual(t):
                if t == 0:
                    for h, c0 in enumerate((0, C // 2)):
                        dve.wait_ge(h_ok, h + 1)
                        ins = nc.vector.tensor_tensor(x1[:, t, c0:c0 + C // 2], x1[:, t, c0:c0 + C // 2],
                                                      h_rows[:, t, c0:c0 + C // 2], ALU.add)
                    ins.then_inc(w_ok, 1)
                    return
                dve.wait_ge(h_ok, t + 2)
                nc.vector.tensor_tensor(x1[:, t, 0:WC], x1[:, t, 0:WC], h_rows[:, t % H_TILES, 0:WC], ALU.add).then_inc(w_ok, 1)

            def second_normalise(u):
                t, c0, c1 = UNITS[u]
                dve.wait_ge(rstd_ok, T + u + 1)
                if c1 - c0 > DVE_NORM[u]:
                    nc.vector.scalar_tensor_tensor(shift[:, t, c0:c1], mean_var[:, T + t, c0:c1, 0], -1.0,
                                                   rstd[:, T + t, c0:c1], ALU.mult, ALU.mult).then_inc(shift_ok, 1)
                for c in range(c0, c0 + DVE_NORM[u]):
                    nc.vector.tensor_scalar(x1[:, t, c], x1[:, t, c], mean_var[:, T + t, c, 0:1], rstd[:, T + t, c:c + 1],
                                            ALU.subtract, ALU.mult).then_inc(y2_ok, 1)

            def second_statistics(u):
                t, c0, c1 = UNITS[u]
                if c0 < WC:
                    dve.wait_ge(w_ok, t + 1)
                if c1 > WC and t >= 1:
                    dve.wait_ge(wp_ok, t)
                statistics(T + u, T + t, x1[:, t], c0, c1)

            def second_moments(u):
                t, c0, c1 = UNITS[u]
                moments(T + u, T + t, c0, c1)

            def second_variance(u):
                t, c0, c1 = UNITS[u]
                variance(T + u, T + t, c0, c1)

            second_residual(0)
            for t in range(T - 1):
                second_statistics(t)
                if t == 0:
                    second_residual(1)
                    second_moments(0)
                    second_residual(2)
                else:
                    if t + DVE_AHEAD < T:
                        second_residual(t + DVE_AHEAD)
                    second_moments(t)
                    second_normalise(t - 1)
                second_variance(t)
            second_statistics(T - 1)
            second_moments(T - 1)
            second_statistics(T)
            second_variance(T - 1)
            second_moments(T)
            second_variance(T)
            second_normalise(T - 2)
            second_normalise(T - 1)
            second_normalise(T)

def kernel(**inputs):
    import numpy as np
    import concourse.bacc as bacc
    from concourse.bass_utils import run_bass_kernel_spmd

    i = {name.removeprefix("L0_"): np.asarray(a) for name, a in inputs.items()}
    x = np.ascontiguousarray(i["attn_x"])
    xt = np.ascontiguousarray(x.reshape(T, D, C, D).transpose(0, 3, 2, 1))

    def packed(*mats):
        return np.ascontiguousarray(np.stack(mats, axis=1))

    cols = packed(i["attn_bq"], i["ffn_bf"], i["ffn_bi"], i["ffn_bc"], i["ffn_in_c"], i["attn_bv"])
    arrays = {
        "x": x,
        "xt": xt,
        "w_kq": np.ascontiguousarray(np.concatenate([i["attn_Wk"].T, i["attn_Wq"].T, cols], axis=1)),
        "w_vo_in": packed(i["attn_Wv"], i["attn_Wo"].T),
        "w_gate": packed(*(i["ffn_" + n].T for n in ("wf", "wi", "wc", "uf", "ui", "uc"))),
        "w_out": packed(i["ffn_wo"].T, i["ffn_uo"].T),
        "rows": np.ascontiguousarray(np.stack([i["attn_bk"], i["ffn_bo"]])),
        "att_row": i["attn_bo"],
    }
    nc = bacc.Bacc("TRN2", target_bir_lowering=False, num_devices=1)
    aps = [nc.dram_tensor(n, a.shape, F32, kind="ExternalInput").ap() for n, a in arrays.items()]
    out = nc.dram_tensor("out", (T, N, D), F32, kind="ExternalOutput").ap()
    build(nc, *aps, out)
    return run_bass_kernel_spmd(nc, [arrays], core_ids=[0]).results[0]["out"]
```
